# Optimizing a Trainium2 kernel written in Bass

```python
import numpy as np
import jax
import jax.numpy as jnp

def _softmax(x, axis=-1):
    return jax.nn.softmax(x, axis=axis)

def _gelu(x):
    return jax.nn.gelu(x, approximate=True)

def _silu(x):
    return jax.nn.silu(x)

def _sigmoid(x):
    return jax.nn.sigmoid(x)

def _layernorm(x, axis=-1, eps=1e-05):
    m = jnp.mean(x, axis=axis, keepdims=True)
    v = jnp.var(x, axis=axis, keepdims=True)
    return (x - m) / jnp.sqrt(v + eps)

def _scatter_add(tgt, idx, src, axis=0):
    return tgt.at[idx].add(src)

def _segment_sum(src, seg, n):
    return jax.ops.segment_sum(src, seg, n)
kernel_name = 'mk_dlrm_tower_d1_rec_r8_6bf48a'

def setup_inputs(seed: int=0):
    np.random.seed(seed)
    _w = jnp.asarray

    def _rec_inputs():
        import jax
        import jax.numpy as jnp
        _tk = jax.random.key(seed)
        dense_ctx = jax.random.normal(jax.random.fold_in(_tk, 190), (512, 16), jnp.float32)
        ids = jnp.stack([jax.random.randint(jax.random.fold_in(_tk, 200 + f), (512,), 0, v, jnp.int32) for f, v in enumerate([12500, 1000, 125000, 1000, 125000, 12500, 1000, 125000, 12500, 1000, 12500, 125000, 125000, 125000, 1250, 1000, 125000, 1000, 1250, 12500, 125000, 12500, 125000, 125000, 1000, 1000, 125000, 1000, 1250, 125000, 12500, 125000, 12500, 12500, 12500, 125000, 12500, 12500, 1000])], axis=1)
        tbl_0 = 0.05 * jax.random.normal(jax.random.fold_in(_tk, 500 + 0), (12500, 16), jnp.float32)
        tbl_1 = 0.05 * jax.random.normal(jax.random.fold_in(_tk, 500 + 1), (1000, 16), jnp.float32)
        tbl_2 = 0.05 * jax.random.normal(jax.random.fold_in(_tk, 500 + 2), (125000, 16), jnp.float32)
        tbl_3 = 0.05 * jax.random.normal(jax.random.fold_in(_tk, 500 + 3), (1000, 16), jnp.float32)
        tbl_4 = 0.05 * jax.random.normal(jax.random.fold_in(_tk, 500 + 4), (125000, 16), jnp.float32)
        tbl_5 = 0.05 * jax.random.normal(jax.random.fold_in(_tk, 500 + 5), (12500, 16), jnp.float32)
        tbl_6 = 0.05 * jax.random.normal(jax.random.fold_in(_tk, 500 + 6), (1000, 16), jnp.float32)
        tbl_7 = 0.05 * jax.random.normal(jax.random.fold_in(_tk, 500 + 7), (125000, 16), jnp.float32)
        tbl_8 = 0.05 * jax.random.normal(jax.random.fold_in(_tk, 500 + 8), (12500, 16), jnp.float32)
        tbl_9 = 0.05 * jax.random.normal(jax.random.fold_in(_tk, 500 + 9), (1000, 16), jnp.float32)
        tbl_10 = 0.05 * jax.random.normal(jax.random.fold_in(_tk, 500 + 10), (12500, 16), jnp.float32)
        tbl_11 = 0.05 * jax.random.normal(jax.random.fold_in(_tk, 500 + 11), (125000, 16), jnp.float32)
        tbl_12 = 0.05 * jax.random.normal(jax.random.fold_in(_tk, 500 + 12), (125000, 16), jnp.float32)
        tbl_13 = 0.05 * jax.random.normal(jax.random.fold_in(_tk, 500 + 13), (125000, 16), jnp.float32)
        tbl_14 = 0.05 * jax.random.normal(jax.random.fold_in(_tk, 500 + 14), (1250, 16), jnp.float32)
        tbl_15 = 0.05 * jax.random.normal(jax.random.fold_in(_tk, 500 + 15), (1000, 16), jnp.float32)
        tbl_16 = 0.05 * jax.random.normal(jax.random.fold_in(_tk, 500 + 16), (125000, 16), jnp.float32)
        tbl_17 = 0.05 * jax.random.normal(jax.random.fold_in(_tk, 500 + 17), (1000, 16), jnp.float32)
        tbl_18 = 0.05 * jax.random.normal(jax.random.fold_in(_tk, 500 + 18), (1250, 16), jnp.float32)
        tbl_19 = 0.05 * jax.random.normal(jax.random.fold_in(_tk, 500 + 19), (12500, 16), jnp.float32)
        tbl_20 = 0.05 * jax.random.normal(jax.random.fold_in(_tk, 500 + 20), (125000, 16), jnp.float32)
        tbl_21 = 0.05 * jax.random.normal(jax.random.fold_in(_tk, 500 + 21), (12500, 16), jnp.float32)
        tbl_22 = 0.05 * jax.random.normal(jax.random.fold_in(_tk, 500 + 22), (125000, 16), jnp.float32)
        tbl_23 = 0.05 * jax.random.normal(jax.random.fold_in(_tk, 500 + 23), (125000, 16), jnp.float32)
        tbl_24 = 0.05 * jax.random.normal(jax.random.fold_in(_tk, 500 + 24), (1000, 16), jnp.float32)
        tbl_25 = 0.05 * jax.random.normal(jax.random.fold_in(_tk, 500 + 25), (1000, 16), jnp.float32)
        tbl_26 = 0.05 * jax.random.normal(jax.random.fold_in(_tk, 500 + 26), (125000, 16), jnp.float32)
        tbl_27 = 0.05 * jax.random.normal(jax.random.fold_in(_tk, 500 + 27), (1000, 16), jnp.float32)
        tbl_28 = 0.05 * jax.random.normal(jax.random.fold_in(_tk, 500 + 28), (1250, 16), jnp.float32)
        tbl_29 = 0.05 * jax.random.normal(jax.random.fold_in(_tk, 500 + 29), (125000, 16), jnp.float32)
        tbl_30 = 0.05 * jax.random.normal(jax.random.fold_in(_tk, 500 + 30), (12500, 16), jnp.float32)
        tbl_31 = 0.05 * jax.random.normal(jax.random.fold_in(_tk, 500 + 31), (125000, 16), jnp.float32)
        tbl_32 = 0.05 * jax.random.normal(jax.random.fold_in(_tk, 500 + 32), (12500, 16), jnp.float32)
        tbl_33 = 0.05 * jax.random.normal(jax.random.fold_in(_tk, 500 + 33), (12500, 16), jnp.float32)
        tbl_34 = 0.05 * jax.random.normal(jax.random.fold_in(_tk, 500 + 34), (12500, 16), jnp.float32)
        tbl_35 = 0.05 * jax.random.normal(jax.random.fold_in(_tk, 500 + 35), (125000, 16), jnp.float32)
        tbl_36 = 0.05 * jax.random.normal(jax.random.fold_in(_tk, 500 + 36), (12500, 16), jnp.float32)
        tbl_37 = 0.05 * jax.random.normal(jax.random.fold_in(_tk, 500 + 37), (12500, 16), jnp.float32)
        tbl_38 = 0.05 * jax.random.normal(jax.random.fold_in(_tk, 500 + 38), (1000, 16), jnp.float32)
        _rk = jax.random.fold_in(_tk, 7)
        W_top1 = 0.05 * jax.random.normal(jax.random.fold_in(_tk, 801), (400, 512), jnp.float32)
        W_top2 = 0.0441942 * jax.random.normal(jax.random.fold_in(_tk, 802), (512, 256), jnp.float32)
        W_top3 = 0.0625 * jax.random.normal(jax.random.fold_in(_tk, 803), (256, 1), jnp.float32)
        b_top1 = jnp.zeros((512,), jnp.float32)
        b_top2 = jnp.zeros((256,), jnp.float32)
        return (dense_ctx, ids, tbl_0, tbl_1, tbl_2, tbl_3, tbl_4, tbl_5, tbl_6, tbl_7, tbl_8, tbl_9, tbl_10, tbl_11, tbl_12, tbl_13, tbl_14, tbl_15, tbl_16, tbl_17, tbl_18, tbl_19, tbl_20, tbl_21, tbl_22, tbl_23, tbl_24, tbl_25, tbl_26, tbl_27, tbl_28, tbl_29, tbl_30, tbl_31, tbl_32, tbl_33, tbl_34, tbl_35, tbl_36, tbl_37, tbl_38, W_top1, b_top1, W_top2, b_top2, W_top3)
    dense_ctx, ids, tbl_0, tbl_1, tbl_2, tbl_3, tbl_4, tbl_5, tbl_6, tbl_7, tbl_8, tbl_9, tbl_10, tbl_11, tbl_12, tbl_13, tbl_14, tbl_15, tbl_16, tbl_17, tbl_18, tbl_19, tbl_20, tbl_21, tbl_22, tbl_23, tbl_24, tbl_25, tbl_26, tbl_27, tbl_28, tbl_29, tbl_30, tbl_31, tbl_32, tbl_33, tbl_34, tbl_35, tbl_36, tbl_37, tbl_38, W_top1, b_top1, W_top2, b_top2, W_top3 = _rec_inputs()

    def _L0_rec_setup():
        import jax, jax.numpy as jnp
        import numpy as np
        B, F0, D = (512, 39, 16)
        CIN = [128, 128, 128]

        def _cin_layer(X0, Xi, W, b):
            H = W.shape[0]
            F0_, Fi = (X0.shape[1], Xi.shape[1])
            Wr = W.reshape(H, F0_, Fi)
            return jnp.einsum('hjk,bjd,bkd->bhd', Wr, X0, Xi) + b[None, :, None]
        key = jax.random.key(seed)
        ks = jax.random.split(key, 4)
        x = jax.random.normal(ks[0], (B, F0, D), dtype=jnp.float32)
        fields = [F0] + CIN
        inp = {'embedded_features': x}
        for i in range(len(CIN)):
            cin = F0 * fields[i]
            cout = fields[i + 1]
            kw = jax.random.fold_in(ks[1], i)
            inp[f'W{i}'] = jax.random.normal(kw, (cout, cin), dtype=jnp.float32) / np.sqrt(cin)
            inp[f'b{i}'] = jnp.zeros((cout,), dtype=jnp.float32)
        return inp
    _L0_rec_all = _L0_rec_setup()
    _L0_rec_in = {k: v for k, v in _L0_rec_all.items() if k in ('W0', 'b0', 'W1', 'b1', 'W2', 'b2')}
    del _L0_rec_all
    return {'dense_ctx': dense_ctx, 'ids': ids, 'tbl_0': tbl_0, 'tbl_1': tbl_1, 'tbl_2': tbl_2, 'tbl_3': tbl_3, 'tbl_4': tbl_4, 'tbl_5': tbl_5, 'tbl_6': tbl_6, 'tbl_7': tbl_7, 'tbl_8': tbl_8, 'tbl_9': tbl_9, 'tbl_10': tbl_10, 'tbl_11': tbl_11, 'tbl_12': tbl_12, 'tbl_13': tbl_13, 'tbl_14': tbl_14, 'tbl_15': tbl_15, 'tbl_16': tbl_16, 'tbl_17': tbl_17, 'tbl_18': tbl_18, 'tbl_19': tbl_19, 'tbl_20': tbl_20, 'tbl_21': tbl_21, 'tbl_22': tbl_22, 'tbl_23': tbl_23, 'tbl_24': tbl_24, 'tbl_25': tbl_25, 'tbl_26': tbl_26, 'tbl_27': tbl_27, 'tbl_28': tbl_28, 'tbl_29': tbl_29, 'tbl_30': tbl_30, 'tbl_31': tbl_31, 'tbl_32': tbl_32, 'tbl_33': tbl_33, 'tbl_34': tbl_34, 'tbl_35': tbl_35, 'tbl_36': tbl_36, 'tbl_37': tbl_37, 'tbl_38': tbl_38, 'W_top1': W_top1, 'b_top1': b_top1, 'W_top2': W_top2, 'b_top2': b_top2, 'W_top3': W_top3, 'L0_rec_W0': _L0_rec_in['W0'], 'L0_rec_b0': _L0_rec_in['b0'], 'L0_rec_W1': _L0_rec_in['W1'], 'L0_rec_b1': _L0_rec_in['b1'], 'L0_rec_W2': _L0_rec_in['W2'], 'L0_rec_b2': _L0_rec_in['b2']}

def reference(dense_ctx, ids, tbl_0, tbl_1, tbl_2, tbl_3, tbl_4, tbl_5, tbl_6, tbl_7, tbl_8, tbl_9, tbl_10, tbl_11, tbl_12, tbl_13, tbl_14, tbl_15, tbl_16, tbl_17, tbl_18, tbl_19, tbl_20, tbl_21, tbl_22, tbl_23, tbl_24, tbl_25, tbl_26, tbl_27, tbl_28, tbl_29, tbl_30, tbl_31, tbl_32, tbl_33, tbl_34, tbl_35, tbl_36, tbl_37, tbl_38, W_top1, b_top1, W_top2, b_top2, W_top3, L0_rec_W0, L0_rec_b0, L0_rec_W1, L0_rec_b1, L0_rec_W2, L0_rec_b2):
    import jax
    import jax.numpy as jnp

    def _L0_rec_ref(embedded_features, W0, b0, W1, b1, W2, b2):
        import jax, jax.numpy as jnp
        import numpy as np
        B, F0, D = (512, 39, 16)
        CIN = [128, 128, 128]

        def _cin_layer(X0, Xi, W, b):
            H = W.shape[0]
            F0_, Fi = (X0.shape[1], Xi.shape[1])
            Wr = W.reshape(H, F0_, Fi)
            return jnp.einsum('hjk,bjd,bkd->bhd', Wr, X0, Xi) + b[None, :, None]
        X0 = embedded_features
        Ws = [(W0, b0), (W1, b1), (W2, b2)]
        Xi = X0
        res = []
        for W, b in Ws:
            Xi = _cin_layer(X0, Xi, W, b)
            res.append(Xi.sum(axis=2))
        return jnp.concatenate(res, axis=1)
    e = jnp.stack([tbl_0[ids[:, 0]], tbl_1[ids[:, 1]], tbl_2[ids[:, 2]], tbl_3[ids[:, 3]], tbl_4[ids[:, 4]], tbl_5[ids[:, 5]], tbl_6[ids[:, 6]], tbl_7[ids[:, 7]], tbl_8[ids[:, 8]], tbl_9[ids[:, 9]], tbl_10[ids[:, 10]], tbl_11[ids[:, 11]], tbl_12[ids[:, 12]], tbl_13[ids[:, 13]], tbl_14[ids[:, 14]], tbl_15[ids[:, 15]], tbl_16[ids[:, 16]], tbl_17[ids[:, 17]], tbl_18[ids[:, 18]], tbl_19[ids[:, 19]], tbl_20[ids[:, 20]], tbl_21[ids[:, 21]], tbl_22[ids[:, 22]], tbl_23[ids[:, 23]], tbl_24[ids[:, 24]], tbl_25[ids[:, 25]], tbl_26[ids[:, 26]], tbl_27[ids[:, 27]], tbl_28[ids[:, 28]], tbl_29[ids[:, 29]], tbl_30[ids[:, 30]], tbl_31[ids[:, 31]], tbl_32[ids[:, 32]], tbl_33[ids[:, 33]], tbl_34[ids[:, 34]], tbl_35[ids[:, 35]], tbl_36[ids[:, 36]], tbl_37[ids[:, 37]], tbl_38[ids[:, 38]]], axis=1)
    z = _L0_rec_ref(e, L0_rec_W0, L0_rec_b0, L0_rec_W1, L0_rec_b1, L0_rec_W2, L0_rec_b2)
    z = z.reshape(z.shape[0], -1)
    h = jnp.concatenate([z, dense_ctx], axis=1)
    h = jnp.maximum(h @ W_top1 + b_top1, 0.0)
    h = jnp.maximum(h @ W_top2 + b_top2, 0.0)
    y = h @ W_top3
    return y

_drawn_inputs = setup_inputs


def setup_inputs(seed=0):
    import zlib

    import numpy as np

    out = dict(_drawn_inputs(seed))
    spreads = {'b_top1': (0.0, 0.1),
     'b_top2': (0.0, 0.1),
     'L0_rec_b0': (0.0, 0.1),
     'L0_rec_b1': (0.0, 0.1),
     'L0_rec_b2': (0.0, 0.1)}
    factors = {'tbl_0': 8.0,
     'tbl_1': 5.868,
     'tbl_2': 5.364,
     'tbl_3': 6.789,
     'tbl_4': 8.0,
     'tbl_5': 8.0,
     'tbl_6': 8.0,
     'tbl_7': 6.86,
     'tbl_8': 8.0,
     'tbl_9': 8.0,
     'tbl_10': 8.0,
     'tbl_11': 6.856,
     'tbl_12': 8.0,
     'tbl_13': 8.0,
     'tbl_14': 4.286,
     'tbl_15': 5.528,
     'tbl_16': 8.0,
     'tbl_17': 8.0,
     'tbl_18': 8.0,
     'tbl_19': 6.095,
     'tbl_20': 7.27,
     'tbl_21': 8.0,
     'tbl_22': 8.0,
     'tbl_23': 8.0,
     'tbl_24': 8.0,
     'tbl_25': 7.318,
     'tbl_26': 6.029,
     'tbl_27': 8.0,
     'tbl_28': 8.0,
     'tbl_29': 8.0,
     'tbl_30': 6.613,
     'tbl_31': 6.39,
     'tbl_32': 8.0,
     'tbl_33': 6.508,
     'tbl_34': 8.0,
     'tbl_35': 7.584,
     'tbl_36': 8.0,
     'tbl_37': 6.34,
     'tbl_38': 8.0,
     'L0_rec_W0': 3.206}
    for name, (base, spread) in spreads.items():
        noise = np.random.default_rng([zlib.crc32(name.encode()), seed]).standard_normal(out[name].shape)
        drawn = base * np.exp(spread * noise) if base else spread * noise
        out[name] = jnp.asarray(drawn.astype(out[name].dtype))
    for name, factor in factors.items():
        out[name] = (out[name] * factor).astype(out[name].dtype)
    return out
```

```python
import concourse.bass as bass
from concourse import mybir
from contextlib import ExitStack

FP32 = mybir.dt.float32
FP32R = mybir.dt.float32r
BF16 = mybir.dt.bfloat16
INT32 = mybir.dt.int32
ALU = mybir.AluOpType
ACT = mybir.ActivationFunctionType
AX = mybir.AxisListType

B, F, D, H, CTX = 512, 39, 16, 128, 16
TOP1, TOP2 = 512, 256
BLOCK_B, MACRO_B, TILE_B = 128, 32, 8
BLOCKS = B // BLOCK_B
MACROS = BLOCK_B // MACRO_B
TILES = MACRO_B // TILE_B
COLS = MACRO_B * D
SHIFTS = (F + 1) // 2
STACK = 3
ROWS = STACK * F
GROUPS = -(-SHIFTS // STACK)
GROUP_ROWS = [F * min(STACK, SHIFTS - STACK * k) for k in range(GROUPS)]
QUADS = 10
S_COLUMNS, S_FACTOR = 1, 4
S_PAIR = [7 + 3 * k for k in range(GROUPS)]
S_ADD = [s + 5 for s in S_PAIR]
S_SPLIT, S_TRANSPOSE = 27, (31, 35)
Q_LAYER2 = 3
S_Z3, S_Z3_STEP, S_H1, S_H2, S_Y = 15, 5, 25, 29, 33
QUAD_J = [list(range(36, 39))] + [list(range(4 * q, 4 * q + 4)) for q in range(9)]
SLOTS = TILES * QUADS
RING = 4
GJ = F + 1
C1 = TOP1 // 128
C2 = TOP2 // 128
W1_PARTS = 3

U_BLOCK = MACROS * SLOTS
TILES_BLOCK = MACROS * TILES
GATHER_BLOCK = 16 * F
CHAIN_TILE = 20
A_TILE = 5
GATHER_TILES = 10
SUM_TILE = 4


def need(engine, sem, value):
    if isinstance(value, int) and value <= 0:
        return
    engine.wait_ge(sem, value)


def build(nc, tables, ids, consts_bf, mask_d, w0_d, w1_d, w2_d, b1_d, cols_d, wt1_d, wt2_d, ctx_d, out):
    with ExitStack() as ctx:
        def sb(name, shape, dt=FP32):
            return ctx.enter_context(nc.sbuf_tensor(name, shape, dt))

        def bank(name):
            return ctx.enter_context(nc.psum_tensor(name, [128, 512], FP32))

        def sem(name):
            return ctx.enter_context(nc.semaphore(name))

        idx = sb("idx", [128, F], INT32)
        emb = sb("emb", [128, F * D])
        rest = sb("rest", [128, D, F])
        parts = sb("parts", [128, D, ROWS], BF16)
        x0s = sb("x0s", [ROWS, BLOCK_B, D], BF16)
        consts = sb("consts", [128, 128 + (GROUPS + 1) * ROWS + F], BF16)
        ident = consts[:, 0:128]
        sel_a_w = consts[0:ROWS, 128:128 + ROWS]
        sel_b_w = [consts[0:ROWS, 128 + (k + 1) * ROWS:128 + (k + 1) * ROWS + GROUP_ROWS[k]]
                   for k in range(GROUPS)]
        sel_i = consts[0:ROWS, 128 + (GROUPS + 1) * ROWS:128 + (GROUPS + 1) * ROWS + F]
        mask = sb("mask", [128, TILE_B])
        w0ab = sb("w0ab", [ROWS, 2, GROUPS, H])
        w0 = sb("w0", [ROWS, GROUPS, H])
        w1h = sb("w1h", [H, F * H], FP32R)
        w1l = sb("w1l", [H, F * H], FP32R)
        w2 = sb("w2", [H, F, H])
        g_all = sb("g_all", [H, GJ, BLOCK_B])
        w1_raw = g_all[:, 0:F, :].rearrange("k j h -> k (j h)")
        b1 = sb("b1", [128, H])
        cols = sb("cols", [128, C1 + 2 * C2 + 2])
        b2d = sb("b2d", [128, 1])
        wt1 = sb("wt1", [128, 3, TOP1])
        wt1c = sb("wt1c", [CTX, TOP1])
        wt2 = sb("wt2", [128, C1, TOP2])
        ctxt = sb("ctxt", [CTX, B])
        fac_a = sb("fac_a", [ROWS, COLS])
        z0 = sb("z0", [ROWS, 2, COLS])
        x1f = sb("x1f", [H, COLS])
        x1h = sb("x1h", [H, 2, COLS], FP32R)
        x1l = sb("x1l", [H, 2, COLS], FP32R)
        x0t = sb("x0t", [128, 2, TILES, GJ])
        bd = sb("bd", [128, TILES, TILE_B, GJ])
        start = sb("start", [128, 2, 3, H])
        prod = sb("prod", [128, 2, 4, 4 * H])
        psum_a = sb("psum_a", [128, 2, 4 * H])
        chain = sb("chain", [128, 2, 4, H])
        total = sb("total", [128, 2, 4 * H])
        half = sb("half", [128, 2 * H])
        x2t = sb("x2t", [128, 2, H])
        z1 = sb("z1", [H, B])
        z2 = sb("z2", [H, BLOCK_B])
        z3 = sb("z3", [H, BLOCK_B])
        h1 = sb("h1", [128, C1, BLOCK_B])
        h2 = sb("h2", [128, C2, BLOCK_B])
        y = sb("y", [1, B])
        bt1 = [cols[:, c:c + 1] for c in range(C1)]
        bt2 = [cols[:, C1 + c:C1 + c + 1] for c in range(C2)]
        wt3 = [cols[:, C1 + C2 + c:C1 + C2 + c + 1] for c in range(C2)]
        b0 = cols[:, C1 + 2 * C2:C1 + 2 * C2 + 1]
        b2 = cols[:, C1 + 2 * C2 + 1:C1 + 2 * C2 + 2]

        p_u = [bank(f"p_u{i}") for i in range(RING)]
        p_sel = bank("p_sel")
        p_x1 = bank("p_x1")
        p_g = bank("p_g")
        p_z = bank("p_z")
        p_tr = p_z[0:ROWS, :].bitcast(BF16)

        idx_in = sem("idx_in")
        consts_in = sem("consts_in")
        mask_in = sem("mask_in")
        w0_in = sem("w0_in")
        w1_in = [sem(f"w1_in{i}") for i in range(W1_PARTS)]
        w2_in = sem("w2_in")
        b1_in = sem("b1_in")
        cols_in = sem("cols_in")
        tower_in = sem("tower_in")
        gathered = sem("gathered")
        ones_set = sem("ones_set")
        w0_summed = sem("w0_summed")
        w1h_made = sem("w1h_made")
        w1l_made = sem("w1l_made")
        b2d_made = sem("b2d_made")
        split_step = sem("split_step")
        tr_full = sem("tr_full")
        x0s_made = sem("x0s_made")
        xt_full = sem("xt_full")
        x0t_made = sem("x0t_made")
        a_full = sem("a_full")
        a_made = sem("a_made")
        b_full = sem("b_full")
        z0_made = sem("z0_made")
        l0_added = sem("l0_added")
        x1f_made = sem("x1f_made")
        x1h_made = sem("x1h_made")
        x1l_made = sem("x1l_made")
        z1_made = sem("z1_made")
        bd_made = sem("bd_made")
        u_full = sem("u_full")
        a_scaled = sem("a_scaled")
        chained = sem("chained")
        summed = sem("summed")
        halved = sem("halved")
        x2_made = sem("x2_made")
        g_full = sem("g_full")
        g_kept = sem("g_kept")
        z3_full = sem("z3_full")
        z3_made = sem("z3_made")
        h1_full = sem("h1_full")
        h1_made = sem("h1_made")
        h2_full = sem("h2_full")
        h2_made = sem("h2_made")
        y_full = sem("y_full")
        y_made = sem("y_made")
        stored = sem("stored")

        block = ctx.enter_context(nc.Block())

        def over_blocks(engine, body):
            body(0, False, True)
            with engine.Fori(1, BLOCKS - 1) as n:
                body(n, True, True)
            body(BLOCKS - 1, True, False)

        @block.sync
        def _(sp):
            sp.dma_start(idx[:], ids[0]).then_inc(idx_in, 16)
            sp.dma_start(consts[:], consts_bf).then_inc(consts_in, 16)
            step = F * H // W1_PARTS
            for i in range(W1_PARTS):
                sp.dma_start(w1_raw[:, i * step:(i + 1) * step], w1_d[:, i * step:(i + 1) * step]).then_inc(w1_in[i], 16)
            sp.dma_start(w0ab[:].rearrange("p a k h -> p (a k h)"), w0_d).then_inc(w0_in, 16)
            sp.dma_start(cols[:], cols_d).then_inc(cols_in, 16)
            sp.dma_start(mask[:], mask_d).then_inc(mask_in, 16)
            sp.dma_start(b1[:], b1_d).then_inc(b1_in, 16)
            sp.dma_start(w2[:].rearrange("k j h -> k (j h)"), w2_d).then_inc(w2_in, 16)
            sp.dma_start(wt1[:], wt1_d[0:3 * 128, :].rearrange("(c p) n -> p c n", p=128)).then_inc(tower_in, 16)
            sp.dma_start(wt1c[:], wt1_d[3 * 128:3 * 128 + CTX, :]).then_inc(tower_in, 16)
            sp.dma_start(wt2[:], wt2_d.rearrange("(c p) n -> p c n", p=128)).then_inc(tower_in, 16)
            sp.dma_start(ctxt[:], ctx_d).then_inc(tower_in, 16)
            with sp.Fori(1, BLOCKS) as n:
                sp.wait_ge(gathered, n * GATHER_BLOCK)
                sp.dma_start(idx[:], ids[n]).then_inc(idx_in, 16)
            sp.wait_ge(y_made, BLOCKS)
            sp.dma_start(out.rearrange("b a -> a b"), y[:]).then_inc(stored, 16)
            sp.wait_ge(stored, 16)

        @block.gpsimd
        def _(pool):
            def gather(f):
                nc.gpsimd.indirect_dma_start(
                    out=emb[:, f * D:(f + 1) * D], out_offset=None, in_=tables[f],
                    in_offset=bass.IndirectOffsetOnAxis(ap=idx[:, 0 + f:f + 1], axis=0)).then_inc(gathered, 16)

            def body(n, has_prev, has_next):
                sent = 0
                for tt in range(TILES_BLOCK):
                    T = n * TILES_BLOCK + tt
                    p = tt % 2
                    if has_next and tt == 0:
                        pool.wait_ge(idx_in, 16 * n + 32)
                        pool.wait_ge(split_step, 4 * n + 4)
                    pool.wait_ge(a_scaled, A_TILE * T + 3)
                    need(pool, summed, SUM_TILE * (T - 1))
                    nc.gpsimd.tensor_tensor(out=psum_a[:, p, :], in0=prod[:, p, 0, :], in1=prod[:, p, 1, :],
                                            op=ALU.add).then_inc(summed, 1)
                    if has_next:
                        upto = min(F, -(-F * (tt + 1) // GATHER_TILES))
                        while sent < upto:
                            gather(sent)
                            sent += 1
                    for i in (2, 3):
                        pool.wait_ge(a_scaled, A_TILE * T + 2 + i)
                        pool.wait_ge(summed, SUM_TILE * T + i - 1)
                        nc.gpsimd.tensor_tensor(out=psum_a[:, p, :], in0=psum_a[:, p, :], in1=prod[:, p, i, :],
                                                op=ALU.add).then_inc(summed, 1)
                    pool.wait_ge(summed, SUM_TILE * T + 3)
                    pool.wait_ge(chained, CHAIN_TILE * (T + 1))
                    need(pool, halved, T - 1)
                    nc.gpsimd.tensor_tensor(out=total[:, p, :], in0=psum_a[:, p, :],
                                            in1=chain[:, p].rearrange("p a h -> p (a h)"),
                                            op=ALU.add).then_inc(summed, 1)

            pool.wait_ge(idx_in, 16)
            for f in range(F):
                gather(f)
            over_blocks(pool, body)

        @block.scalar
        def _(act):
            def evac_tr(n, r):
                need(act, b_full, MACROS * GROUPS * n)
                need(act, xt_full, MACROS * n)
                act.wait_ge(tr_full, 2 * n + r + 1)
                nc.scalar.activation(x0s[:, :, 8 * r:8 * r + 8],
                                     p_tr.rearrange("p (d b) -> p b d", d=8), ACT.Copy).then_inc(x0s_made, 1)

            def evac_x0t(M, par):
                act.wait_ge(xt_full, M + 1)
                need(act, chained, CHAIN_TILE * TILES * (M - 1))
                need(act, a_scaled, A_TILE * TILES * (M - 1))
                need(act, bd_made, TILES * (M - 1))
                nc.scalar.activation(x0t[:, par, :, 0:F],
                                     p_sel[:, 0:TILES * GJ].rearrange("p (t j) -> p t j", j=GJ)[:, :, 0:F],
                                     ACT.Copy).then_inc(x0t_made, 1)

            def evac_a(M):
                act.wait_ge(a_full, M + 1)
                need(act, z0_made, GROUPS * M)
                nc.scalar.activation(fac_a[:], p_sel[0:ROWS, :], ACT.Copy).then_inc(a_made, 1)

            def evac_x1(M, par):
                act.wait_ge(l0_added, GROUPS * (M + 1))
                need(act, z1_made, M)
                need(act, x1l_made, M)
                need(act, x1h_made, M)
                nc.scalar.activation(x1f[:], p_x1[:], ACT.Identity, bias=b0).then_inc(x1f_made, 1)

            def make_x1h(M, par):
                act.wait_ge(x1f_made, M + 1)
                need(act, u_full, SLOTS * (M - 1))
                nc.scalar.activation(x1h[:, par, :], x1f[:], ACT.Copy).then_inc(x1h_made, 1)

            def keep_g(T, tt):
                act.wait_ge(g_full, T + 1)
                nc.scalar.activation(g_all[:, :, TILE_B * tt:TILE_B * (tt + 1)],
                                     p_g[:, 0:TILE_B * GJ].rearrange("h (b j) -> h j b", j=GJ),
                                     ACT.Copy).then_inc(g_kept, 1)

            def scale_quad(T, tt, q):
                p, par, t = tt % 2, (tt // TILES) % 2, tt % TILES
                act.wait_ge(u_full, QUADS * T + q + 1)
                if q == 0:
                    need(act, chained, CHAIN_TILE * (T - 2) + 4)
                    dst = start[:, p].rearrange("p a h -> p (a h)")
                else:
                    need(act, summed, SUM_TILE * (T - 2) + 3)
                    dst = prod[:, p, q // 2 - 1, :]
                u = p_u[(QUADS * tt + q) % RING]
                for i, j in enumerate(QUAD_J[q]):
                    last = nc.scalar.activation(dst[:, i * H:(i + 1) * H], u[:, i * H:(i + 1) * H], ACT.Copy,
                                                scale=x0t[:, par, t, j:j + 1])
                last.then_inc(a_scaled, 1)

            def tower_z(n):
                act.wait_ge(z3_full, n + 1)
                need(act, h1_full, n)
                nc.scalar.activation(z3[:], p_z[:, 0:BLOCK_B], ACT.Identity, bias=b2d[:]).then_inc(z3_made, 1)
                act.wait_ge(g_kept, TILES_BLOCK * (n + 1))
                nc.scalar.activation(z2[:], g_all[:, F, :], ACT.Copy).then_inc(z3_made, 1)

            def tower_h1(n):
                act.wait_ge(h1_full, n + 1)
                need(act, h2_full, n)
                for c in range(C1):
                    nc.scalar.activation(h1[:, c, :], p_z[:, c * BLOCK_B:(c + 1) * BLOCK_B], ACT.Relu,
                                         bias=bt1[c]).then_inc(h1_made, 1)

            def tower_h2(n):
                act.wait_ge(h2_full, n + 1)
                need(act, y_full, n)
                for c in range(C2):
                    nc.scalar.activation(h2[:, c, :], p_z[:, c * BLOCK_B:(c + 1) * BLOCK_B], ACT.Relu,
                                         bias=bt2[c]).then_inc(h2_made, 1)

            def tower_y(n):
                act.wait_ge(y_full, n + 1)
                nc.scalar.activation(y[0:1, bass.ds(BLOCK_B * n, BLOCK_B)], p_z[0:1, 0:BLOCK_B],
                                     ACT.Copy).then_inc(y_made, 1)

            def body(n, has_prev, has_next):
                for m in range(MACROS):
                    M = n * MACROS + m
                    prepares = has_next or m < MACROS - 1
                    act.wait_ge(x0t_made, M + 1)
                    for s in range(SLOTS):
                        tt = m * TILES + s // QUADS
                        q = s % QUADS
                        T = n * TILES_BLOCK + tt
                        if has_next and m == MACROS - 2 and s in S_TRANSPOSE:
                            evac_tr(n + 1, S_TRANSPOSE.index(s))
                        if prepares and s == S_COLUMNS:
                            evac_x0t(M + 1, (m + 1) % 2)
                        if prepares and s == S_FACTOR:
                            evac_a(M + 1)
                        if prepares and s == S_ADD[-1]:
                            evac_x1(M + 1, (m + 1) % 2)
                            make_x1h(M + 1, (m + 1) % 2)
                        if q == Q_LAYER2 and (has_prev or tt > 1):
                            if tt == 2:
                                need(act, z3_made, 2 * n)
                            keep_g(T - 2, (tt - 2) % TILES_BLOCK)
                        if has_prev and m == 0:
                            if s == S_Z3 + 7:
                                tower_z(n - 1)
                            if s == S_H1:
                                tower_h1(n - 1)
                            if s == S_H2:
                                tower_h2(n - 1)
                            if s == S_Y:
                                tower_y(n - 1)
                        if q % 2 == 0:
                            scale_quad(T, tt, q)

            step = F * H // W1_PARTS
            for i in range(W1_PARTS):
                act.wait_ge(w1_in[i], 16)
                nc.scalar.activation(w1h[:, i * step:(i + 1) * step], w1_raw[:, i * step:(i + 1) * step],
                                     ACT.Copy).then_inc(w1h_made, 1)
            act.wait_ge(cols_in, 16)
            nc.scalar.mul(b2d[:], b2, float(D)).then_inc(b2d_made, 1)
            act.wait_ge(b2d_made, 1)
            act.wait_ge(ones_set, 1)
            evac_tr(0, 0)
            evac_tr(0, 1)
            evac_x0t(0, 0)
            evac_a(0)
            evac_x1(0, 0)
            make_x1h(0, 0)
            act.wait_ge(w1l_made, W1_PARTS)
            over_blocks(act, body)
            n = BLOCKS - 1
            for tt in (TILES_BLOCK - 2, TILES_BLOCK - 1):
                keep_g(TILES_BLOCK * n + tt, tt)
            tower_z(n)
            tower_h1(n)
            tower_h2(n)
            tower_y(n)

        @block.vector
        def _(dve):
            def split_block(n):
                rows = emb[:].rearrange("p (j d) -> p d j", d=D)
                dve.wait_ge(gathered, GATHER_BLOCK * (n + 1))
                need(dve, tr_full, 2 * n)
                nc.vector.tensor_copy(parts[:, :, 0:F], rows).then_inc(split_step, 1)
                dve.wait_ge(split_step, 4 * n + 1)
                nc.vector.tensor_tensor(out=rest[:], in0=rows, in1=parts[:, :, 0:F],
                                        op=ALU.subtract).then_inc(split_step, 1)
                dve.wait_ge(split_step, 4 * n + 2)
                nc.vector.tensor_copy(parts[:, :, F:2 * F], rest[:]).then_inc(split_step, 1)
                dve.wait_ge(split_step, 4 * n + 3)
                nc.vector.tensor_tensor(out=parts[:, :, 2 * F:3 * F], in0=rest[:], in1=parts[:, :, F:2 * F],
                                        op=ALU.subtract).then_inc(split_step, 1)

            def product(M, k):
                rows = GROUP_ROWS[k]
                dve.wait_ge(a_made, M + 1)
                dve.wait_ge(b_full, GROUPS * M + k + 1)
                need(dve, l0_added, GROUPS * M + max(k - 1, 0))
                nc.vector.tensor_tensor(out=z0[0:rows, k % 2, :], in0=p_sel[0:rows, :], in1=fac_a[0:rows, :],
                                        op=ALU.mult).then_inc(z0_made, 1)

            def make_x1l(M, par):
                dve.wait_ge(x1h_made, M + 1)
                need(dve, u_full, SLOTS * (M - 1))
                nc.vector.tensor_tensor(out=x1l[:, par, :], in0=x1f[:], in1=x1h[:, par, :].bitcast(FP32),
                                        op=ALU.subtract).then_inc(x1l_made, 1)
                nc.vector.tensor_reduce(out=z1[:, bass.ds(M * MACRO_B, MACRO_B)],
                                        in_=x1f[:].rearrange("h (b d) -> h b d", d=D),
                                        op=ALU.add, axis=AX.X).then_inc(z1_made, 1)

            def make_bd(T, tt):
                par, t = (tt // TILES) % 2, tt % TILES
                need(dve, g_full, T - 3)
                nc.vector.tensor_tensor(
                    out=bd[:, t], in0=x0t[:, par, t].unsqueeze(1).to_broadcast([128, TILE_B, GJ]),
                    in1=mask[:].unsqueeze(2).to_broadcast([128, TILE_B, GJ]), op=ALU.mult).then_inc(bd_made, 1)

            def chain_quad(T, tt, q):
                p, par, t = tt % 2, (tt // TILES) % 2, tt % TILES
                k = q // 2
                dve.wait_ge(u_full, QUADS * T + q + 1)
                if k == 0:
                    dve.wait_ge(a_scaled, A_TILE * T + 1)
                    need(dve, summed, SUM_TILE * (T - 1))
                u = p_u[(QUADS * tt + q) % RING]
                for i, j in enumerate(QUAD_J[q]):
                    if k == 0:
                        add = b1[:] if i == 0 else start[:, p, i - 1, :]
                    else:
                        add = chain[:, p, i, :]
                        dve.wait_ge(chained, CHAIN_TILE * T + 4 * (k - 1) + i + 1)
                    nc.vector.scalar_tensor_tensor(
                        out=chain[:, p, i, :], in0=u[:, i * H:(i + 1) * H], scalar=x0t[:, par, t, j:j + 1],
                        in1=add, op0=ALU.mult, op1=ALU.add).then_inc(chained, 1)

            def fold_half(T, p):
                dve.wait_ge(summed, SUM_TILE * (T + 1))
                need(dve, x2_made, T)
                nc.vector.tensor_tensor(out=half[:], in0=total[:, p, 0:2 * H], in1=total[:, p, 2 * H:4 * H],
                                        op=ALU.add).then_inc(halved, 1)

            def fold_x2(T, p):
                dve.wait_ge(halved, T + 1)
                need(dve, g_full, T - 1)
                nc.vector.tensor_tensor(out=x2t[:, p, :], in0=half[:, 0:H], in1=half[:, H:2 * H],
                                        op=ALU.add).then_inc(x2_made, 1)

            def body(n, has_prev, has_next):
                for m in range(MACROS):
                    M = n * MACROS + m
                    prepares = has_next or m < MACROS - 1
                    dve.wait_ge(x0t_made, M + 1)
                    for s in range(SLOTS):
                        tt = m * TILES + s // QUADS
                        q = s % QUADS
                        T = n * TILES_BLOCK + tt
                        if q == 9:
                            make_bd(T, tt)
                        if q == 5 and (has_prev or tt > 0):
                            fold_half(T - 1, (tt + 1) % 2)
                        if q == 7 and (has_prev or tt > 0):
                            fold_x2(T - 1, (tt + 1) % 2)
                        if has_next and m == MACROS - 2 and s == S_SPLIT:
                            split_block(n + 1)
                        for k in range(GROUPS):
                            if prepares and s == S_PAIR[k]:
                                product(M + 1, k)
                        if prepares and s == S_ADD[-1] + 1:
                            make_x1l(M + 1, (m + 1) % 2)
                        if q % 2 == 1:
                            chain_quad(T, tt, q)

            nc.vector.memset(x0t[:], 1.0).then_inc(ones_set, 1)
            dve.wait_ge(w0_in, 16)
            nc.vector.tensor_tensor(out=w0[:], in0=w0ab[:, 0], in1=w0ab[:, 1], op=ALU.add).then_inc(w0_summed, 1)
            step = F * H // W1_PARTS
            for i in range(W1_PARTS):
                dve.wait_ge(w1h_made, i + 1)
                nc.vector.tensor_tensor(out=w1l[:, i * step:(i + 1) * step], in0=w1_raw[:, i * step:(i + 1) * step],
                                        in1=w1h[:, i * step:(i + 1) * step].bitcast(FP32),
                                        op=ALU.subtract).then_inc(w1l_made, 1)
            dve.wait_ge(mask_in, 16)
            dve.wait_ge(b1_in, 16)
            split_block(0)
            for k in range(GROUPS):
                product(0, k)
            make_x1l(0, 0)
            over_blocks(dve, body)
            T = TILES_BLOCK * BLOCKS - 1
            fold_half(T, T % 2)
            fold_x2(T, T % 2)

        @block.tensor
        def _(pe):
            def transposes(n, r):
                pe.wait_ge(split_step, 4 * n + 4)
                need(pe, x0s_made, 2 * n + r)
                need(pe, y_made, n - 1)
                for d in range(8):
                    last = nc.tensor.transpose(p_tr[:, 128 * d:128 * (d + 1)], parts[:, 8 * r + d, :], ident)
                last.then_inc(tr_full, 1)

            def columns_on_partitions(n, m, M):
                pe.wait_ge(x0s_made, 2 * n + 2)
                need(pe, z0_made, GROUPS * M)
                for t in range(TILES):
                    b = m * MACRO_B + t * TILE_B
                    last = nc.tensor.matmul(p_sel[:, t * GJ:t * GJ + F],
                                            x0s[:, b:b + TILE_B, :].rearrange("p b d -> p (b d)"), sel_i,
                                            start=True, stop=True)
                last.then_inc(xt_full, 1)

            def x0_cols(m):
                return x0s[:, m * MACRO_B:(m + 1) * MACRO_B, :].rearrange("p b d -> p (b d)")

            def select_a(M, m):
                pe.wait_ge(x0t_made, M + 1)
                nc.tensor.matmul(p_sel[0:ROWS, :], sel_a_w, x0_cols(m), start=True, stop=True).then_inc(a_full, 1)

            def select_b(M, m, k):
                if k == 0:
                    pe.wait_ge(a_made, M + 1)
                else:
                    pe.wait_ge(z0_made, GROUPS * M + k)
                nc.tensor.matmul(p_sel[0:GROUP_ROWS[k], :], sel_b_w[k], x0_cols(m),
                                 start=True, stop=True).then_inc(b_full, 1)

            def add_group(M, k):
                pe.wait_ge(z0_made, GROUPS * M + k + 1)
                if k == 0:
                    need(pe, x1f_made, M)
                nc.tensor.matmul(p_x1[:], w0[0:GROUP_ROWS[k], k, :], z0[0:GROUP_ROWS[k], k % 2, :],
                                 start=(k == 0), stop=(k == GROUPS - 1)).then_inc(l0_added, 1)

            def quad(T, tt, q):
                par, t = (tt // TILES) % 2, tt % TILES
                if q % 2 == 0:
                    need(pe, a_scaled, A_TILE * T + q // 2 - 1)
                else:
                    need(pe, chained, CHAIN_TILE * T + 4 * (q // 2 - 1))
                js = QUAD_J[q]
                u = p_u[(QUADS * tt + q) % RING][:, 0:len(js) * H]
                xh = x1h[:, par, t * 128:(t + 1) * 128]
                xl = x1l[:, par, t * 128:(t + 1) * 128]
                wh = w1h[:, js[0] * H:(js[-1] + 1) * H]
                wl = w1l[:, js[0] * H:(js[-1] + 1) * H]
                nc.tensor.matmul(u, xh, wh, start=True, stop=False)
                nc.tensor.matmul(u, xh, wl, start=False, stop=False)
                nc.tensor.matmul(u, xl, wh, start=False, stop=True).then_inc(u_full, 1)

            def layer2(T, tt):
                t, p = tt % TILES, tt % 2
                pe.wait_ge(x2_made, T + 1)
                pe.wait_ge(bd_made, T + 1)
                need(pe, g_kept, T)
                nc.tensor.matmul(p_g[:, 0:TILE_B * GJ], x2t[:, p, :], bd[:, t].rearrange("p b j -> p (b j)"),
                                 start=True, stop=True).then_inc(g_full, 1)

            def tower_z3(n, j0, j1):
                if j0 == 0:
                    pe.wait_ge(g_kept, TILES_BLOCK * (n + 1))
                    pe.wait_ge(w2_in, 16)
                for j in range(j0, j1):
                    last = nc.tensor.matmul(p_z[:, 0:BLOCK_B], w2[:, j, :], g_all[:, j, :],
                                            start=(j == 0), stop=(j == F - 1))
                if j1 == F:
                    last.then_inc(z3_full, 1)

            def tower_1(n):
                pe.wait_ge(z3_made, 2 * (n + 1))
                pe.wait_ge(tower_in, 64)
                pe.wait_ge(z1_made, MACROS * (n + 1))
                for c in range(C1):
                    o = p_z[:, c * BLOCK_B:(c + 1) * BLOCK_B]
                    w = slice(c * 128, (c + 1) * 128)
                    nc.tensor.matmul(o, wt1[:, 0, w], z1[:, bass.ds(BLOCK_B * n, BLOCK_B)], start=True, stop=False)
                    nc.tensor.matmul(o, wt1[:, 1, w], z2[:], start=False, stop=False)
                    nc.tensor.matmul(o, wt1[:, 2, w], z3[:], start=False, stop=False)
                    last = nc.tensor.matmul(o, wt1c[:, w], ctxt[:, bass.ds(BLOCK_B * n, BLOCK_B)],
                                            start=False, stop=True)
                last.then_inc(h1_full, 1)

            def tower_2(n):
                pe.wait_ge(h1_made, C1 * (n + 1))
                for c in range(C2):
                    for i in range(C1):
                        last = nc.tensor.matmul(p_z[:, c * BLOCK_B:(c + 1) * BLOCK_B], wt2[:, i, c * 128:(c + 1) * 128],
                                                h1[:, i, :], start=(i == 0), stop=(i == C1 - 1))
                last.then_inc(h2_full, 1)

            def tower_3(n):
                pe.wait_ge(h2_made, C2 * (n + 1))
                for i in range(C2):
                    last = nc.tensor.matmul(p_z[0:1, 0:BLOCK_B], wt3[i], h2[:, i, :], start=(i == 0), stop=(i == C2 - 1))
                last.then_inc(y_full, 1)

            def prepare(n, m, M, s):
                if s == S_COLUMNS:
                    columns_on_partitions(n, m, M)
                if s == S_FACTOR:
                    select_a(M, m)
                for k in range(GROUPS):
                    if s == S_ADD[k]:
                        add_group(M, k)
                    if s == S_PAIR[k]:
                        select_b(M, m, k)

            def body(n, has_prev, has_next):
                for m in range(MACROS):
                    M = n * MACROS + m
                    pe.wait_ge(x1h_made, M + 1)
                    pe.wait_ge(x1l_made, M + 1)
                    for s in range(SLOTS):
                        tt = m * TILES + s // QUADS
                        q = s % QUADS
                        T = n * TILES_BLOCK + tt
                        if m < MACROS - 1:
                            prepare(n, m + 1, M + 1, s)
                        elif has_next:
                            prepare(n + 1, 0, M + 1, s)
                        if has_next and m == MACROS - 2 and s in S_TRANSPOSE:
                            transposes(n + 1, S_TRANSPOSE.index(s))
                        if q == Q_LAYER2 and (has_prev or tt > 1):
                            layer2(T - 2, (tt - 2) % TILES_BLOCK)
                        if has_prev and m == 0:
                            if S_Z3 <= s < S_Z3 + 8:
                                tower_z3(n - 1, S_Z3_STEP * (s - S_Z3), min(F, S_Z3_STEP * (s - S_Z3 + 1)))
                            if s == S_H1:
                                tower_1(n - 1)
                            if s == S_H2:
                                tower_2(n - 1)
                            if s == S_Y:
                                tower_3(n - 1)
                        quad(T, tt, q)

            pe.wait_ge(consts_in, 16)
            pe.wait_ge(w0_summed, 1)
            transposes(0, 0)
            transposes(0, 1)
            columns_on_partitions(0, 0, 0)
            select_a(0, 0)
            for k in range(GROUPS):
                select_b(0, 0, k)
                add_group(0, k)
            pe.wait_ge(w1l_made, W1_PARTS)
            over_blocks(pe, body)
            n = BLOCKS - 1
            T = TILES_BLOCK * BLOCKS - 1
            for tt in (TILES_BLOCK - 2, TILES_BLOCK - 1):
                layer2(TILES_BLOCK * n + tt, tt)
            tower_z3(n, 0, F)
            tower_1(n)
            tower_2(n)
            tower_3(n)


def _stacked_selectors(np):
    picks = []
    for k in range(-1, GROUPS):
        m = np.zeros((128, ROWS), np.float32)
        for r in range(ROWS):
            shift = 0 if k < 0 else STACK * k + r // F
            m[np.arange(STACK) * F + (r % F + shift) % F, r] = 1
        picks.append(m)
    plain = np.zeros((128, F), np.float32)
    for j in range(F):
        plain[np.arange(STACK) * F + j, j] = 1
    return np.concatenate([np.eye(128, dtype=np.float32), *picks, plain], axis=1)


def kernel(**inputs):
    import ml_dtypes
    import numpy as np
    import concourse.bacc as bacc
    from concourse.bass_utils import run_bass_kernel_spmd

    x = {k: np.asarray(v) for k, v in inputs.items()}
    f32 = np.float32
    shift = np.arange(SHIFTS)[:, None]
    j = np.arange(F)[None, :]
    k = (j + shift) % F
    w0 = x["L0_rec_W0"].reshape(H, F, F)
    w0ab = np.zeros((STACK * GROUPS, F, 2, H), f32)
    w0ab[:SHIFTS, :, 0] = w0[:, j + 0 * shift, k].transpose(1, 2, 0)
    w0ab[1:SHIFTS, :, 1] = w0[:, k[1:], (j + 0 * shift)[1:]].transpose(1, 2, 0)
    w0ab = w0ab.reshape(GROUPS, ROWS, 2, H).transpose(1, 2, 0, 3).reshape(ROWS, 2 * GROUPS * H)
    w_j = {n: x[f"L0_rec_W{n}"].reshape(H, F, H).transpose(2, 1, 0).reshape(H, F * H) for n in (1, 2)}
    cols = np.concatenate([x["b_top1"].reshape(C1, 128).T, x["b_top2"].reshape(C2, 128).T,
                           x["W_top3"].reshape(C2, 128).T, x["L0_rec_b0"][:, None], x["L0_rec_b2"][:, None]], axis=1)
    arrays = {
        "ids": x["ids"].reshape(BLOCKS, BLOCK_B, F),
        "consts": _stacked_selectors(np).astype(ml_dtypes.bfloat16),
        "mask": (np.arange(128)[:, None] // D == np.arange(TILE_B)[None, :]).astype(f32),
        "w0ab": w0ab, "w1": w_j[1], "w2": w_j[2],
        "b1": np.broadcast_to(x["L0_rec_b1"], (128, H)),
        "cols": cols, "wt1": x["W_top1"], "wt2": x["W_top2"], "ctx": x["dense_ctx"].T,
    }
    arrays = {k + "_in": np.ascontiguousarray(v) for k, v in arrays.items()}
    tables = {f"tbl_{f}": np.ascontiguousarray(x[f"tbl_{f}"]) for f in range(F)}
    nc = bacc.Bacc("TRN2", target_bir_lowering=False, num_devices=1)

    def declare(name, a):
        return nc.dram_tensor(name, a.shape, mybir.dt.from_np(a.dtype), kind="ExternalInput").ap()

    table_aps = [declare(name, a) for name, a in tables.items()]
    args = [declare(name, a) for name, a in arrays.items()]
    out = nc.dram_tensor("out", (B, 1), FP32, kind="ExternalOutput").ap()
    build(nc, table_aps, *args, out)
    result = run_bass_kernel_spmd(nc, [{**tables, **arrays}], core_ids=[0])
    return result.results[0]["out"]
```

```python
import concourse.bass as bass
from concourse import mybir
from contextlib import ExitStack

FP32 = mybir.dt.float32
FP32R = mybir.dt.float32r
BF16 = mybir.dt.bfloat16
INT32 = mybir.dt.int32
ALU = mybir.AluOpType
ACT = mybir.ActivationFunctionType
AX = mybir.AxisListType

B, F, D, H, CTX = 512, 39, 16, 128, 16
TOP1, TOP2 = 512, 256
BLOCK_B, MACRO_B, TILE_B = 128, 32, 8
BLOCKS = B // BLOCK_B
MACROS = BLOCK_B // MACRO_B
TILES = MACRO_B // TILE_B
COLS = MACRO_B * D
SHIFTS = (F + 1) // 2
STACK = 3
ROWS = STACK * F
GROUPS = -(-SHIFTS // STACK)
GROUP_ROWS = [F * min(STACK, SHIFTS - STACK * k) for k in range(GROUPS)]
Z_RING = 3
QUADS = 10
GATHERS = -(-MACRO_B // STACK)
G_BATCH = [range(4, 8), range(8, GATHERS), (), range(0, 4)]
G_AHEAD = [2, 2, 3, 3]
GATHER_ROWS = [F * sum(c * GATHERS + g < MACRO_B for c in range(STACK)) for g in range(GATHERS)]
PICK_COLS = [D * min(GATHERS, MACRO_B - c * GATHERS) for c in range(STACK)]
S_FACTOR, S_COLUMNS = 0, 2
S_PAIR = [2 + 4 * k for k in range(GROUPS)]
S_HIGH = [s + 3 for s in S_PAIR] 
S_LOW = [s + 5 for s in S_PAIR]
S_ADD = [s + 8 for s in S_PAIR]
S_SPLIT = [29, 31, 32, 33]
S_PICK = 36
S_Z1 = 1
Q_LAYER2 = 3
S_Z3, S_Z3_STEP, S_H1, S_H2, S_Y = 15, 5, 25, 29, 33
QUAD_J = [list(range(36, 39))] + [list(range(4 * q, 4 * q + 4)) for q in range(9)]
SLOTS = TILES * QUADS
RING = 4
GJ = F + 1
C1 = TOP1 // 128
C2 = TOP2 // 128
W1_PARTS = 3

U_BLOCK = MACROS * SLOTS
TILES_BLOCK = MACROS * TILES
CHAIN_TILE = 20
A_TILE = 5
SUM_TILE = 4


def need(engine, sem, value):
    if isinstance(value, int) and value <= 0:
        return
    engine.wait_ge(sem, value)


def build(nc, table, ids, base_d, consts_bf, mask_d, w0_d, w1_d, w2_d, b1_d, cols_d, wt1_d, wt2_d, ctx_d, out):
    with ExitStack() as ctx:
        def sb(name, shape, dt=FP32):
            return ctx.enter_context(nc.sbuf_tensor(name, shape, dt))

        def bank(name):
            return ctx.enter_context(nc.psum_tensor(name, [128, 512], FP32))

        def sem(name):
            return ctx.enter_context(nc.semaphore(name))

        row_of = sb("row_of", [ROWS, MACROS * BLOCKS * GATHERS], INT32)
        base = sb("base", [ROWS, MACROS * BLOCKS * GATHERS], INT32)
        idx_all = sb("idx_all", [ROWS, MACROS * BLOCKS * GATHERS], INT32)
        idx = sb("idx", [ROWS, GATHERS], INT32)
        emb = sb("emb", [ROWS, GATHERS * D])
        rest = sb("rest", [ROWS, GATHERS * D])
        parts = sb("parts", [ROWS, STACK, GATHERS * D], BF16)
        x0s = sb("x0s", [ROWS, COLS], BF16)
        consts = sb("consts", [128, (STACK * STACK + GROUPS + 1) * ROWS + F], BF16)

        def selector(i, width):
            return consts[0:ROWS, i * ROWS:i * ROWS + width]

        pick = [[selector(STACK * c + part, ROWS) for part in range(STACK)] for c in range(STACK)]
        sel_a = selector(STACK * STACK, ROWS)
        sel_b = [selector(STACK * STACK + 1 + k, GROUP_ROWS[k]) for k in range(GROUPS)]
        sel_i = selector(STACK * STACK + 1 + GROUPS, F)
        mask = sb("mask", [128, TILE_B])
        w0ab = sb("w0ab", [ROWS, 2, GROUPS, H])
        w0 = sb("w0", [ROWS, GROUPS, H])
        w0h = sb("w0h", [ROWS, GROUPS, H], FP32R)
        w0l = sb("w0l", [ROWS, GROUPS, H], FP32R)
        w1h = sb("w1h", [H, F * H], FP32R)
        w1l = sb("w1l", [H, F * H], FP32R)
        w2 = sb("w2", [H, F, H])
        g_all = sb("g_all", [H, GJ, BLOCK_B])
        w1_raw = g_all[:, 0:F, :].rearrange("k j h -> k (j h)")
        b1 = sb("b1", [128, H])
        cols = sb("cols", [128, C1 + 2 * C2 + 2])
        b2d = sb("b2d", [128, 1])
        wt1 = sb("wt1", [128, 3, TOP1])
        wt1c = sb("wt1c", [CTX, TOP1])
        wt2 = sb("wt2", [128, C1, TOP2])
        ctxt = sb("ctxt", [CTX, B])
        fac_a = sb("fac_a", [ROWS, COLS])
        z0 = sb("z0", [ROWS, Z_RING, COLS])
        z0h = sb("z0h", [ROWS, Z_RING, COLS], FP32R)
        z0l = sb("z0l", [ROWS, Z_RING, COLS], FP32R)
        x1f = sb("x1f", [H, COLS])
        x1h = sb("x1h", [H, 2, COLS], FP32R)
        x1l = sb("x1l", [H, 2, COLS], FP32R)
        x0t = sb("x0t", [128, 2, TILES, GJ])
        bd = sb("bd", [128, TILES, TILE_B, GJ])
        start = sb("start", [128, 2, 3, H])
        prod = sb("prod", [128, 2, 4, 4 * H])
        psum_a = sb("psum_a", [128, 2, 4 * H])
        chain = sb("chain", [128, 2, 4, H])
        total = sb("total", [128, 2, 4 * H])
        half = sb("half", [128, 2 * H])
        x2t = sb("x2t", [128, 2, H])
        z1 = sb("z1", [H, B])
        z2 = sb("z2", [H, BLOCK_B])
        z3 = sb("z3", [H, BLOCK_B])
        h1 = sb("h1", [128, C1, BLOCK_B])
        h2 = sb("h2", [128, C2, BLOCK_B])
        y = sb("y", [1, B])
        bt1 = [cols[:, c:c + 1] for c in range(C1)]
        bt2 = [cols[:, C1 + c:C1 + c + 1] for c in range(C2)]
        wt3 = [cols[:, C1 + C2 + c:C1 + C2 + c + 1] for c in range(C2)]
        b0 = cols[:, C1 + 2 * C2:C1 + 2 * C2 + 1]
        b2 = cols[:, C1 + 2 * C2 + 1:C1 + 2 * C2 + 2]

        p_u = [bank(f"p_u{i}") for i in range(RING)]
        p_sel = bank("p_sel")
        p_x1 = bank("p_x1")
        p_g = bank("p_g")
        p_z = bank("p_z")

        idx_in = sem("idx_in")
        consts_in = sem("consts_in")
        mask_in = sem("mask_in")
        w0_in = sem("w0_in")
        w1_in = [sem(f"w1_in{i}") for i in range(W1_PARTS)]
        w2_in = sem("w2_in")
        b1_in = sem("b1_in")
        cols_in = sem("cols_in")
        tower_in = sem("tower_in")
        idx_made = sem("idx_made")
        emb_cleared = sem("emb_cleared")
        idx_copied = sem("idx_copied")
        gathered = sem("gathered")
        ones_set = sem("ones_set")
        w0_summed = sem("w0_summed")
        w0h_made = sem("w0h_made")
        w0l_made = sem("w0l_made")
        w1h_made = sem("w1h_made")
        w1l_made = sem("w1l_made")
        b2d_made = sem("b2d_made")
        split_step = sem("split_step")
        picked = sem("picked")
        x0s_made = sem("x0s_made")
        xt_full = sem("xt_full")
        x0t_made = sem("x0t_made")
        a_full = sem("a_full")
        a_made = sem("a_made")
        b_full = sem("b_full")
        z0_made = sem("z0_made")
        z0h_made = sem("z0h_made")
        z0l_made = sem("z0l_made")
        l0_added = sem("l0_added")
        x1f_made = sem("x1f_made")
        x1h_made = sem("x1h_made")
        x1l_made = sem("x1l_made")
        z1_made = sem("z1_made")
        bd_made = sem("bd_made")
        u_full = sem("u_full")
        a_scaled = sem("a_scaled")
        chained = sem("chained")
        summed = sem("summed")
        halved = sem("halved")
        x2_made = sem("x2_made")
        g_full = sem("g_full")
        g_kept = sem("g_kept")
        z3_full = sem("z3_full")
        z3_made = sem("z3_made")
        h1_full = sem("h1_full")
        h1_made = sem("h1_made")
        h2_full = sem("h2_full")
        h2_made = sem("h2_made")
        y_full = sem("y_full")
        y_made = sem("y_made")
        stored = sem("stored")

        block = ctx.enter_context(nc.Block())

        def over_blocks(engine, body):
            body(0, False, True)
            with engine.Fori(1, BLOCKS - 1) as n:
                body(n, True, True)
            body(BLOCKS - 1, True, False)

        @block.sync
        def _(sp):
            sp.dma_start(row_of[:], ids).then_inc(idx_in, 16)
            sp.dma_start(base[:], base_d).then_inc(idx_in, 16)
            sp.dma_start(consts[:], consts_bf).then_inc(consts_in, 16)
            step = F * H // W1_PARTS
            for i in range(W1_PARTS):
                sp.dma_start(w1_raw[:, i * step:(i + 1) * step], w1_d[:, i * step:(i + 1) * step]).then_inc(w1_in[i], 16)
            sp.dma_start(w0ab[:].rearrange("p a k h -> p (a k h)"), w0_d).then_inc(w0_in, 16)
            sp.dma_start(cols[:], cols_d).then_inc(cols_in, 16)
            sp.dma_start(mask[:], mask_d).then_inc(mask_in, 16)
            sp.dma_start(b1[:], b1_d).then_inc(b1_in, 16)
            sp.wait_ge(gathered, 16 * GATHERS)
            sp.dma_start(w2[:].rearrange("k j h -> k (j h)"), w2_d).then_inc(w2_in, 16)
            sp.dma_start(wt1[:], wt1_d[0:3 * 128, :].rearrange("(c p) n -> p c n", p=128)).then_inc(tower_in, 16)
            sp.dma_start(wt1c[:], wt1_d[3 * 128:3 * 128 + CTX, :]).then_inc(tower_in, 16)
            sp.dma_start(wt2[:], wt2_d.rearrange("(c p) n -> p c n", p=128)).then_inc(tower_in, 16)
            sp.dma_start(ctxt[:], ctx_d).then_inc(tower_in, 16)
            sp.wait_ge(y_made, BLOCKS)
            sp.dma_start(out.rearrange("b a -> a b"), y[:]).then_inc(stored, 16)
            sp.wait_ge(stored, 16)

        @block.gpsimd
        def _(pool):
            def gather(g, index):
                rows = GATHER_ROWS[g]
                nc.gpsimd.indirect_dma_start(
                    out=emb[0:rows, g * D:(g + 1) * D], out_offset=None, in_=table,
                    in_offset=bass.IndirectOffsetOnAxis(ap=index[0:rows, g:g + 1], axis=0)).then_inc(gathered, 16)

            def body(n, has_prev, has_next):
                for tt in range(TILES_BLOCK):
                    T = n * TILES_BLOCK + tt
                    p, m, t = tt % 2, tt // TILES, tt % TILES
                    pool.wait_ge(a_scaled, A_TILE * T + 3)
                    need(pool, summed, SUM_TILE * (T - 1))
                    nc.gpsimd.tensor_tensor(out=psum_a[:, p, :], in0=prod[:, p, 0, :], in1=prod[:, p, 1, :],
                                            op=ALU.add).then_inc(summed, 1)
                    for i in (2, 3):
                        pool.wait_ge(a_scaled, A_TILE * T + 2 + i)
                        pool.wait_ge(summed, SUM_TILE * T + i - 1)
                        nc.gpsimd.tensor_tensor(out=psum_a[:, p, :], in0=psum_a[:, p, :], in1=prod[:, p, i, :],
                                                op=ALU.add).then_inc(summed, 1)
                    pool.wait_ge(summed, SUM_TILE * T + 3)
                    pool.wait_ge(chained, CHAIN_TILE * (T + 1))
                    need(pool, halved, T - 1)
                    gathers = has_next or m < MACROS - G_AHEAD[t]
                    if gathers and G_BATCH[t] and G_BATCH[t][0] == 0:
                        M = n * MACROS + m + G_AHEAD[t]
                        pool.wait_ge(idx_copied, M - 1)
                        pool.wait_ge(split_step, 4 * M)
                    nc.gpsimd.tensor_tensor(out=total[:, p, :], in0=psum_a[:, p, :],
                                            in1=chain[:, p].rearrange("p a h -> p (a h)"),
                                            op=ALU.add).then_inc(summed, 1)
                    if gathers:
                        for g in G_BATCH[t]:
                            gather(g, idx)

            pool.wait_ge(idx_made, 1)
            pool.wait_ge(emb_cleared, 1)
            for M in (0, 1):
                need(pool, split_step, 4 * M)
                for g in range(GATHERS):
                    gather(g, idx_all[:, GATHERS * M:GATHERS * (M + 1)])
            pool.wait_ge(split_step, 4 * 2)
            pool.wait_ge(idx_copied, 1)
            for g in range(G_BATCH[0][0]):
                gather(g, idx)
            over_blocks(pool, body)

        @block.scalar
        def _(act):
            def split_part(M, step):
                if step == 0:
                    act.wait_ge(gathered, 16 * GATHERS * (M + 1))
                    need(act, picked, M)
                    nc.scalar.activation(parts[:, 0, :], emb[:], ACT.Copy).then_inc(split_step, 1)
                else:
                    act.wait_ge(split_step, 4 * M + 2)
                    nc.scalar.activation(parts[:, 1, :], rest[:], ACT.Copy).then_inc(split_step, 1)

            def evac_pick(M):
                act.wait_ge(picked, M + 1)
                need(act, b_full, GROUPS * M)
                nc.scalar.activation(x0s[:], p_z[0:ROWS, :], ACT.Copy).then_inc(x0s_made, 1)

            def evac_x0t(M, par):
                act.wait_ge(xt_full, M + 1)
                need(act, chained, CHAIN_TILE * TILES * (M - 1))
                need(act, a_scaled, A_TILE * TILES * (M - 1))
                need(act, bd_made, TILES * (M - 1))
                nc.scalar.activation(x0t[:, par, :, 0:F],
                                     p_x1[:, 0:TILES * GJ].rearrange("p (t j) -> p t j", j=GJ)[:, :, 0:F],
                                     ACT.Copy).then_inc(x0t_made, 1)

            def evac_a(M):
                act.wait_ge(a_full, M + 1)
                need(act, z0_made, GROUPS * M)
                nc.scalar.activation(fac_a[:], p_sel[0:ROWS, :], ACT.Copy).then_inc(a_made, 1)

            def z0_high(M, k):
                rows = GROUP_ROWS[k]
                act.wait_ge(z0_made, GROUPS * M + k + 1)
                need(act, l0_added, GROUPS * M + max(k - Z_RING + 1, 0))
                nc.scalar.activation(z0h[0:rows, k % Z_RING, :], z0[0:rows, k % Z_RING, :], ACT.Copy).then_inc(z0h_made, 1)

            def evac_x1(M, par):
                act.wait_ge(l0_added, GROUPS * (M + 1))
                need(act, z1_made, M)
                need(act, x1l_made, M)
                need(act, x1h_made, M)
                nc.scalar.activation(x1f[:], p_x1[:], ACT.Identity, bias=b0).then_inc(x1f_made, 1)

            def make_x1h(M, par):
                act.wait_ge(x1f_made, M + 1)
                need(act, u_full, SLOTS * (M - 1))
                nc.scalar.activation(x1h[:, par, :], x1f[:], ACT.Copy).then_inc(x1h_made, 1)

            def keep_g(T, tt):
                act.wait_ge(g_full, T + 1)
                nc.scalar.activation(g_all[:, :, TILE_B * tt:TILE_B * (tt + 1)],
                                     p_g[:, 0:TILE_B * GJ].rearrange("h (b j) -> h j b", j=GJ),
                                     ACT.Copy).then_inc(g_kept, 1)

            def scale_quad(T, tt, q):
                p, par, t = tt % 2, (tt // TILES) % 2, tt % TILES
                act.wait_ge(u_full, QUADS * T + q + 1)
                if q == 0:
                    need(act, chained, CHAIN_TILE * (T - 2) + 4)
                    dst = start[:, p].rearrange("p a h -> p (a h)")
                else:
                    need(act, summed, SUM_TILE * (T - 2) + 3)
                    dst = prod[:, p, q // 2 - 1, :]
                u = p_u[(QUADS * tt + q) % RING]
                for i, j in enumerate(QUAD_J[q]):
                    last = nc.scalar.activation(dst[:, i * H:(i + 1) * H], u[:, i * H:(i + 1) * H], ACT.Copy,
                                                scale=x0t[:, par, t, j:j + 1])
                last.then_inc(a_scaled, 1)

            def tower_z(n):
                act.wait_ge(z3_full, n + 1)
                need(act, h1_full, n)
                nc.scalar.activation(z3[:], p_z[:, 0:BLOCK_B], ACT.Identity, bias=b2d[:]).then_inc(z3_made, 1)
                act.wait_ge(g_kept, TILES_BLOCK * (n + 1))
                nc.scalar.activation(z2[:], g_all[:, F, :], ACT.Copy).then_inc(z3_made, 1)

            def tower_h1(n):
                act.wait_ge(h1_full, n + 1)
                need(act, h2_full, n)
                for c in range(C1):
                    nc.scalar.activation(h1[:, c, :], p_z[:, c * BLOCK_B:(c + 1) * BLOCK_B], ACT.Relu,
                                         bias=bt1[c]).then_inc(h1_made, 1)

            def tower_h2(n):
                act.wait_ge(h2_full, n + 1)
                need(act, y_full, n)
                for c in range(C2):
                    nc.scalar.activation(h2[:, c, :], p_z[:, c * BLOCK_B:(c + 1) * BLOCK_B], ACT.Relu,
                                         bias=bt2[c]).then_inc(h2_made, 1)

            def tower_y(n):
                act.wait_ge(y_full, n + 1)
                nc.scalar.activation(y[0:1, bass.ds(BLOCK_B * n, BLOCK_B)], p_z[0:1, 0:BLOCK_B],
                                     ACT.Copy).then_inc(y_made, 1)

            def body(n, has_prev, has_next):
                for m in range(MACROS):
                    M = n * MACROS + m
                    prepares = has_next or m < MACROS - 1
                    act.wait_ge(x0t_made, M + 1)
                    for s in range(SLOTS):
                        tt = m * TILES + s // QUADS
                        q = s % QUADS
                        T = n * TILES_BLOCK + tt
                        if s in S_SPLIT[0::2] and (has_next or m < MACROS - 2):
                            split_part(M + 2, S_SPLIT.index(s))
                        if s == S_PICK and (has_next or m < MACROS - 2):
                            evac_pick(M + 2)
                        if prepares and s == S_COLUMNS:
                            evac_x0t(M + 1, (m + 1) % 2)
                        if prepares and s == S_FACTOR:
                            evac_a(M + 1)
                        if prepares and s in S_HIGH:
                            z0_high(M + 1, S_HIGH.index(s))
                        if prepares and s == S_ADD[-1]:
                            evac_x1(M + 1, (m + 1) % 2)
                            make_x1h(M + 1, (m + 1) % 2)
                        if q == Q_LAYER2 and (has_prev or tt > 1):
                            if tt == 2:
                                need(act, z3_made, 2 * n)
                            keep_g(T - 2, (tt - 2) % TILES_BLOCK)
                        if has_prev and m == 0:
                            if s == S_Z3 + 7:
                                tower_z(n - 1)
                            if s == S_H1:
                                tower_h1(n - 1)
                            if s == S_H2:
                                tower_h2(n - 1)
                            if s == S_Y:
                                tower_y(n - 1)
                        if q % 2 == 0:
                            scale_quad(T, tt, q)

            act.wait_ge(w0_summed, 1)
            nc.scalar.activation(w0h[:], w0[:], ACT.Copy).then_inc(w0h_made, 1)
            step = F * H // W1_PARTS
            for i in range(W1_PARTS):
                act.wait_ge(w1_in[i], 16)
                nc.scalar.activation(w1h[:, i * step:(i + 1) * step], w1_raw[:, i * step:(i + 1) * step],
                                     ACT.Copy).then_inc(w1h_made, 1)
            act.wait_ge(cols_in, 16)
            nc.scalar.mul(b2d[:], b2, float(D)).then_inc(b2d_made, 1)
            act.wait_ge(b2d_made, 1)
            act.wait_ge(ones_set, 1)
            split_part(0, 0)
            split_part(0, 2)
            evac_pick(0)
            evac_x0t(0, 0)
            evac_a(0)
            for k in range(GROUPS):
                z0_high(0, k)
            evac_x1(0, 0)
            make_x1h(0, 0)
            split_part(1, 0)
            split_part(1, 2)
            evac_pick(1)
            act.wait_ge(w1l_made, W1_PARTS)
            over_blocks(act, body)
            n = BLOCKS - 1
            for tt in (TILES_BLOCK - 2, TILES_BLOCK - 1):
                keep_g(TILES_BLOCK * n + tt, tt)
            tower_z(n)
            tower_h1(n)
            tower_h2(n)
            tower_y(n)

        @block.vector
        def _(dve):
            def split_rest(M, step):
                dve.wait_ge(split_step, 4 * M + step)
                if step == 1:
                    nc.vector.tensor_tensor(out=rest[:], in0=emb[:], in1=parts[:, 0, :],
                                            op=ALU.subtract).then_inc(split_step, 1)
                else:
                    nc.vector.tensor_tensor(out=parts[:, 2, :], in0=rest[:], in1=parts[:, 1, :],
                                            op=ALU.subtract).then_inc(split_step, 1)

            def copy_idx(M):
                nc.vector.tensor_copy(idx[:], idx_all[:, bass.ds(GATHERS * M, GATHERS)]).then_inc(idx_copied, 1)

            def product(M, k):
                rows = GROUP_ROWS[k]
                dve.wait_ge(a_made, M + 1)
                dve.wait_ge(b_full, GROUPS * M + k + 1)
                need(dve, z0l_made, GROUPS * M + max(k - Z_RING + 1, 0))
                nc.vector.tensor_tensor(out=z0[0:rows, k % Z_RING, :], in0=p_sel[0:rows, :], in1=fac_a[0:rows, :],
                                        op=ALU.mult).then_inc(z0_made, 1)

            def z0_low(M, k):
                rows = GROUP_ROWS[k]
                dve.wait_ge(z0h_made, GROUPS * M + k + 1)
                need(dve, l0_added, GROUPS * M + max(k - Z_RING + 1, 0))
                nc.vector.tensor_tensor(out=z0l[0:rows, k % Z_RING, :], in0=z0[0:rows, k % Z_RING, :],
                                        in1=z0h[0:rows, k % Z_RING, :].bitcast(FP32),
                                        op=ALU.subtract).then_inc(z0l_made, 1)

            def make_x1l(M, par):
                dve.wait_ge(x1h_made, M + 1)
                need(dve, u_full, SLOTS * (M - 1))
                nc.vector.tensor_tensor(out=x1l[:, par, :], in0=x1f[:], in1=x1h[:, par, :].bitcast(FP32),
                                        op=ALU.subtract).then_inc(x1l_made, 1)

            def sum_z1(M):
                dve.wait_ge(x1f_made, M + 1)
                nc.vector.tensor_reduce(out=z1[:, bass.ds(M * MACRO_B, MACRO_B)],
                                        in_=x1f[:].rearrange("h (b d) -> h b d", d=D),
                                        op=ALU.add, axis=AX.X).then_inc(z1_made, 1)

            def make_bd(T, tt):
                par, t = (tt // TILES) % 2, tt % TILES
                need(dve, g_full, T - 3)
                nc.vector.tensor_tensor(
                    out=bd[:, t], in0=x0t[:, par, t].unsqueeze(1).to_broadcast([128, TILE_B, GJ]),
                    in1=mask[:].unsqueeze(2).to_broadcast([128, TILE_B, GJ]), op=ALU.mult).then_inc(bd_made, 1)

            def chain_quad(T, tt, q):
                p, par, t = tt % 2, (tt // TILES) % 2, tt % TILES
                k = q // 2
                dve.wait_ge(u_full, QUADS * T + q + 1)
                if k == 0:
                    dve.wait_ge(a_scaled, A_TILE * T + 1)
                    need(dve, summed, SUM_TILE * (T - 1))
                u = p_u[(QUADS * tt + q) % RING]
                for i, j in enumerate(QUAD_J[q]):
                    if k == 0:
                        add = b1[:] if i == 0 else start[:, p, i - 1, :]
                    else:
                        add = chain[:, p, i, :]
                        dve.wait_ge(chained, CHAIN_TILE * T + 4 * (k - 1) + i + 1)
                    nc.vector.scalar_tensor_tensor(
                        out=chain[:, p, i, :], in0=u[:, i * H:(i + 1) * H], scalar=x0t[:, par, t, j:j + 1],
                        in1=add, op0=ALU.mult, op1=ALU.add).then_inc(chained, 1)

            def fold_half(T, p):
                dve.wait_ge(summed, SUM_TILE * (T + 1))
                need(dve, x2_made, T)
                nc.vector.tensor_tensor(out=half[:], in0=total[:, p, 0:2 * H], in1=total[:, p, 2 * H:4 * H],
                                        op=ALU.add).then_inc(halved, 1)

            def fold_x2(T, p):
                dve.wait_ge(halved, T + 1)
                need(dve, g_full, T - 1)
                nc.vector.tensor_tensor(out=x2t[:, p, :], in0=half[:, 0:H], in1=half[:, H:2 * H],
                                        op=ALU.add).then_inc(x2_made, 1)

            def body(n, has_prev, has_next):
                for m in range(MACROS):
                    M = n * MACROS + m
                    prepares = has_next or m < MACROS - 1
                    dve.wait_ge(x0t_made, M + 1)
                    for s in range(SLOTS):
                        tt = m * TILES + s // QUADS
                        q = s % QUADS
                        T = n * TILES_BLOCK + tt
                        if q == 9:
                            make_bd(T, tt)
                        if q == 5 and (has_prev or tt > 0):
                            fold_half(T - 1, (tt + 1) % 2)
                        if q == 7 and (has_prev or tt > 0):
                            fold_x2(T - 1, (tt + 1) % 2)
                        if s == S_Z1:
                            sum_z1(M)
                        if s in S_SPLIT[1::2] and (has_next or m < MACROS - 2):
                            split_rest(M + 2, S_SPLIT.index(s))
                        if s == S_SPLIT[-1] + 1 and (has_next or m < MACROS - 3):
                            copy_idx(M + 3)
                        for k in range(GROUPS):
                            if prepares and s == S_PAIR[k]:
                                product(M + 1, k)
                            if prepares and s == S_LOW[k]:
                                z0_low(M + 1, k)
                        if prepares and s == S_ADD[-1] + 1:
                            make_x1l(M + 1, (m + 1) % 2)
                        if q % 2 == 1:
                            chain_quad(T, tt, q)

            nc.vector.memset(emb[:], 0.0).then_inc(emb_cleared, 1)
            dve.wait_ge(idx_in, 32)
            nc.vector.tensor_tensor(out=idx_all[:], in0=row_of[:], in1=base[:], op=ALU.add).then_inc(idx_made, 1)
            nc.vector.memset(x0t[:], 1.0).then_inc(ones_set, 1)
            dve.wait_ge(w0_in, 16)
            nc.vector.tensor_tensor(out=w0[:], in0=w0ab[:, 0], in1=w0ab[:, 1], op=ALU.add).then_inc(w0_summed, 1)
            dve.wait_ge(w0h_made, 1)
            nc.vector.tensor_tensor(out=w0l[:], in0=w0[:], in1=w0h[:].bitcast(FP32),
                                    op=ALU.subtract).then_inc(w0l_made, 1)
            step = F * H // W1_PARTS
            for i in range(W1_PARTS):
                dve.wait_ge(w1h_made, i + 1)
                nc.vector.tensor_tensor(out=w1l[:, i * step:(i + 1) * step], in0=w1_raw[:, i * step:(i + 1) * step],
                                        in1=w1h[:, i * step:(i + 1) * step].bitcast(FP32),
                                        op=ALU.subtract).then_inc(w1l_made, 1)
            dve.wait_ge(mask_in, 16)
            dve.wait_ge(b1_in, 16)
            split_rest(0, 1)
            split_rest(0, 3)
            dve.wait_ge(idx_made, 1)
            copy_idx(2)
            for k in range(GROUPS):
                product(0, k)
                if k:
                    z0_low(0, k - 1)
            z0_low(0, GROUPS - 1)
            make_x1l(0, 0)
            split_rest(1, 1)
            split_rest(1, 3)
            over_blocks(dve, body)
            T = TILES_BLOCK * BLOCKS - 1
            fold_half(T, T % 2)
            fold_x2(T, T % 2)

        @block.tensor
        def _(pe):
            def pick_rows(M):
                pe.wait_ge(split_step, 4 * (M + 1))
                need(pe, x0s_made, M)
                at = 0
                for c in range(STACK):
                    for part in range(STACK):
                        last = nc.tensor.matmul(p_z[0:ROWS, at:at + PICK_COLS[c]], pick[c][part],
                                                parts[:, part, 0:PICK_COLS[c]],
                                                start=(part == 0), stop=(part == STACK - 1))
                    at += PICK_COLS[c]
                last.then_inc(picked, 1)

            def columns_on_partitions(M):
                pe.wait_ge(x0s_made, M + 1)
                need(pe, x1f_made, M)
                for t in range(TILES):
                    last = nc.tensor.matmul(p_x1[:, t * GJ:t * GJ + F], x0s[:, t * 128:(t + 1) * 128], sel_i,
                                            start=True, stop=True)
                last.then_inc(xt_full, 1)

            def select_a(M):
                pe.wait_ge(x0s_made, M + 1)
                need(pe, z0_made, GROUPS * M)
                nc.tensor.matmul(p_sel[0:ROWS, :], sel_a, x0s[:], start=True, stop=True).then_inc(a_full, 1)

            def select_b(M, k):
                if k == 0:
                    pe.wait_ge(a_made, M + 1)
                else:
                    pe.wait_ge(z0_made, GROUPS * M + k)
                nc.tensor.matmul(p_sel[0:GROUP_ROWS[k], :], sel_b[k], x0s[:],
                                 start=True, stop=True).then_inc(b_full, 1)

            def add_group(M, k):
                rows = GROUP_ROWS[k]
                if k == 0:
                    pe.wait_ge(x0t_made, M + 1)
                wh, wl = w0h[0:rows, k, :], w0l[0:rows, k, :]
                zh, zl = z0h[0:rows, k % Z_RING, :], z0l[0:rows, k % Z_RING, :]
                pe.wait_ge(z0h_made, GROUPS * M + k + 1)
                nc.tensor.matmul(p_x1[:], wh, zh, start=(k == 0), stop=False)
                nc.tensor.matmul(p_x1[:], wl, zh, start=False, stop=False)
                pe.wait_ge(z0l_made, GROUPS * M + k + 1)
                nc.tensor.matmul(p_x1[:], wh, zl, start=False, stop=(k == GROUPS - 1)).then_inc(l0_added, 1)

            def quad(T, tt, q):
                par, t = (tt // TILES) % 2, tt % TILES
                if q % 2 == 0:
                    need(pe, a_scaled, A_TILE * T + q // 2 - 1)
                else:
                    need(pe, chained, CHAIN_TILE * T + 4 * (q // 2 - 1))
                js = QUAD_J[q]
                u = p_u[(QUADS * tt + q) % RING][:, 0:len(js) * H]
                xh = x1h[:, par, t * 128:(t + 1) * 128]
                xl = x1l[:, par, t * 128:(t + 1) * 128]
                wh = w1h[:, js[0] * H:(js[-1] + 1) * H]
                wl = w1l[:, js[0] * H:(js[-1] + 1) * H]
                nc.tensor.matmul(u, xh, wh, start=True, stop=False)
                nc.tensor.matmul(u, xh, wl, start=False, stop=False)
                nc.tensor.matmul(u, xl, wh, start=False, stop=True).then_inc(u_full, 1)

            def layer2(T, tt):
                t, p = tt % TILES, tt % 2
                pe.wait_ge(x2_made, T + 1)
                pe.wait_ge(bd_made, T + 1)
                need(pe, g_kept, T)
                nc.tensor.matmul(p_g[:, 0:TILE_B * GJ], x2t[:, p, :], bd[:, t].rearrange("p b j -> p (b j)"),
                                 start=True, stop=True).then_inc(g_full, 1)

            def tower_z3(n, j0, j1):
                if j0 == 0:
                    pe.wait_ge(g_kept, TILES_BLOCK * (n + 1))
                    pe.wait_ge(w2_in, 16)
                for j in range(j0, j1):
                    last = nc.tensor.matmul(p_z[:, 0:BLOCK_B], w2[:, j, :], g_all[:, j, :],
                                            start=(j == 0), stop=(j == F - 1))
                if j1 == F:
                    last.then_inc(z3_full, 1)

            def tower_1(n):
                pe.wait_ge(z3_made, 2 * (n + 1))
                pe.wait_ge(tower_in, 64)
                pe.wait_ge(z1_made, MACROS * (n + 1))
                for c in range(C1):
                    o = p_z[:, c * BLOCK_B:(c + 1) * BLOCK_B]
                    w = slice(c * 128, (c + 1) * 128)
                    nc.tensor.matmul(o, wt1[:, 0, w], z1[:, bass.ds(BLOCK_B * n, BLOCK_B)], start=True, stop=False)
                    nc.tensor.matmul(o, wt1[:, 1, w], z2[:], start=False, stop=False)
                    nc.tensor.matmul(o, wt1[:, 2, w], z3[:], start=False, stop=False)
                    last = nc.tensor.matmul(o, wt1c[:, w], ctxt[:, bass.ds(BLOCK_B * n, BLOCK_B)],
                                            start=False, stop=True)
                last.then_inc(h1_full, 1)

            def tower_2(n):
                pe.wait_ge(h1_made, C1 * (n + 1))
                for c in range(C2):
                    for i in range(C1):
                        last = nc.tensor.matmul(p_z[:, c * BLOCK_B:(c + 1) * BLOCK_B], wt2[:, i, c * 128:(c + 1) * 128],
                                                h1[:, i, :], start=(i == 0), stop=(i == C1 - 1))
                last.then_inc(h2_full, 1)

            def tower_3(n):
                pe.wait_ge(h2_made, C2 * (n + 1))
                for i in range(C2):
                    last = nc.tensor.matmul(p_z[0:1, 0:BLOCK_B], wt3[i], h2[:, i, :], start=(i == 0), stop=(i == C2 - 1))
                last.then_inc(y_full, 1)

            def prepare(M, s):
                if s == S_COLUMNS:
                    columns_on_partitions(M)
                if s == S_FACTOR:
                    select_a(M)
                for k in range(GROUPS):
                    if s == S_ADD[k]:
                        add_group(M, k)
                    if s == S_PAIR[k]:
                        select_b(M, k)

            def body(n, has_prev, has_next):
                for m in range(MACROS):
                    M = n * MACROS + m
                    pe.wait_ge(x1h_made, M + 1)
                    pe.wait_ge(x1l_made, M + 1)
                    for s in range(SLOTS):
                        tt = m * TILES + s // QUADS
                        q = s % QUADS
                        T = n * TILES_BLOCK + tt
                        if has_next or m < MACROS - 1:
                            prepare(M + 1, s)
                        if s == S_PICK and (has_next or m < MACROS - 2):
                            if m == 0 and has_prev:
                                pe.wait_ge(y_made, n)
                            pick_rows(M + 2)
                        if q == Q_LAYER2 and (has_prev or tt > 1):
                            layer2(T - 2, (tt - 2) % TILES_BLOCK)
                        if has_prev and m == 0:
                            if S_Z3 <= s < S_Z3 + 8:
                                tower_z3(n - 1, S_Z3_STEP * (s - S_Z3), min(F, S_Z3_STEP * (s - S_Z3 + 1)))
                            if s == S_H1:
                                tower_1(n - 1)
                            if s == S_H2:
                                tower_2(n - 1)
                            if s == S_Y:
                                tower_3(n - 1)
                        quad(T, tt, q)

            pe.wait_ge(consts_in, 16)
            pe.wait_ge(w0l_made, 1)
            pick_rows(0)
            columns_on_partitions(0)
            select_a(0)
            for k in range(GROUPS):
                select_b(0, k)
                if k:
                    add_group(0, k - 1)
            add_group(0, GROUPS - 1)
            pick_rows(1)
            pe.wait_ge(w1l_made, W1_PARTS)
            over_blocks(pe, body)
            n = BLOCKS - 1
            T = TILES_BLOCK * BLOCKS - 1
            for tt in (TILES_BLOCK - 2, TILES_BLOCK - 1):
                layer2(TILES_BLOCK * n + tt, tt)
            tower_z3(n, 0, F)
            tower_1(n)
            tower_2(n)
            tower_3(n)


def _selectors(np):
    eye = np.eye(F, dtype=np.float32)
    found = []
    for c in range(STACK):
        for part in range(STACK):
            m = np.zeros((STACK, F, STACK, F), np.float32)
            m[c, :, part] = eye
            found.append(m.reshape(ROWS, ROWS))
    for k in range(-1, GROUPS):
        shifts = [0] * STACK if k < 0 else [STACK * k + i for i in range(STACK)]
        found.append(np.tile(np.concatenate([np.roll(eye, s, axis=0)
                                             for s in shifts], axis=1), (STACK, 1)))
    found.append(np.tile(eye, (STACK, 1)))
    return np.pad(np.concatenate(found, axis=1), ((0, 128 - ROWS), (0, 0)))


def kernel(**inputs):
    import ml_dtypes
    import numpy as np
    import concourse.bacc as bacc
    from concourse.bass_utils import run_bass_kernel_spmd

    x = {k: np.asarray(v) for k, v in inputs.items()}
    f32 = np.float32
    shift = np.arange(SHIFTS)[:, None]
    j = np.arange(F)[None, :]
    k = (j + shift) % F
    w0 = x["L0_rec_W0"].reshape(H, F, F)
    w0ab = np.zeros((STACK * GROUPS, F, 2, H), f32)
    w0ab[:SHIFTS, :, 0] = w0[:, j + 0 * shift, k].transpose(1, 2, 0)
    w0ab[1:SHIFTS, :, 1] = w0[:, k[1:], (j + 0 * shift)[1:]].transpose(1, 2, 0)
    w0ab = w0ab.reshape(GROUPS, ROWS, 2, H).transpose(1, 2, 0, 3).reshape(ROWS, 2 * GROUPS * H)
    w_j = {n: x[f"L0_rec_W{n}"].reshape(H, F, H).transpose(2, 1, 0).reshape(H, F * H) for n in (1, 2)}
    cols = np.concatenate([x["b_top1"].reshape(C1, 128).T, x["b_top2"].reshape(C2, 128).T,
                           x["W_top3"].reshape(C2, 128).T, x["L0_rec_b0"][:, None], x["L0_rec_b2"][:, None]], axis=1)
    sizes = [x[f"tbl_{f}"].shape[0] for f in range(F)]
    samples = np.pad(x["ids"].reshape(-1, MACRO_B, F), ((0, 0), (0, STACK * GATHERS - MACRO_B), (0, 0)))
    ids = samples.reshape(-1, STACK, GATHERS, F).transpose(1, 3, 0, 2).reshape(ROWS, -1)
    first_row = np.concatenate([[0], np.cumsum(sizes)[:-1]]).astype(np.int32)
    base = np.broadcast_to(np.tile(first_row, STACK)[:, None], ids.shape)
    arrays = {
        "table": np.concatenate([x[f"tbl_{f}"] for f in range(F)]),
        "ids": ids, "base": base,
        "consts": _selectors(np).astype(ml_dtypes.bfloat16),
        "mask": (np.arange(128)[:, None] // D == np.arange(TILE_B)[None, :]).astype(f32),
        "w0ab": w0ab, "w1": w_j[1], "w2": w_j[2],
        "b1": np.broadcast_to(x["L0_rec_b1"], (128, H)),
        "cols": cols, "wt1": x["W_top1"], "wt2": x["W_top2"], "ctx": x["dense_ctx"].T,
    }
    arrays = {k + "_in": np.ascontiguousarray(v) for k, v in arrays.items()}
    nc = bacc.Bacc("TRN2", target_bir_lowering=False, num_devices=1)

    def declare(name, a):
        return nc.dram_tensor(name, a.shape, mybir.dt.from_np(a.dtype), kind="ExternalInput").ap()

    args = [declare(name, a) for name, a in arrays.items()]
    out = nc.dram_tensor("out", (B, 1), FP32, kind="ExternalOutput").ap()
    build(nc, *args, out)
    result = run_bass_kernel_spmd(nc, [arrays], core_ids=[0])
    return result.results[0]["out"]
```

```python
import concourse.bass as bass
from concourse import mybir
from contextlib import ExitStack

FP32 = mybir.dt.float32
FP32R = mybir.dt.float32r
INT32 = mybir.dt.int32
ALU = mybir.AluOpType
ACT = mybir.ActivationFunctionType
AX = mybir.AxisListType

B, F, D, H, CTX = 512, 39, 16, 128, 16
TOP1, TOP2 = 512, 256
BLOCK_B, MACRO_B, TILE_B = 128, 32, 8
BLOCKS = B // BLOCK_B
MACROS = BLOCK_B // MACRO_B
TILES = MACRO_B // TILE_B
COLS = MACRO_B * D
SHIFTS = (F + 1) // 2
STACK = 3
ROWS = STACK * F
GROUPS = -(-SHIFTS // STACK)
SHIFT = [[k + GROUPS * i for i in range(STACK)] for k in range(GROUPS)]
GROUP_ROWS = [F * sum(s < SHIFTS for s in SHIFT[k]) for k in range(GROUPS)]
XX_ROWS = ROWS + GROUPS - 1
Z_RING = 3
QUADS = 10
GATHERS = -(-MACRO_B // STACK)
GATHER_ROWS = [F * sum(c * GATHERS + g < MACRO_B for c in range(STACK)) for g in range(GATHERS)]
STAGE_COLS = [D * min(GATHERS, MACRO_B - c * GATHERS) for c in range(STACK)]
G_BATCH = [range(8, GATHERS), (), range(0, 4), range(4, 8)]
G_AHEAD = [2, 2, 3, 3]

S_COLUMNS = 2
S_PAIR = [1 + 9 * k // 2 for k in range(GROUPS)]
S_HIGH = [s + 2 for s in S_PAIR]
S_LOW = [s + 3 for s in S_PAIR]
S_ADD = [s + 6 for s in S_PAIR]
S_INDEX = 25
S_Z1 = 1
Q_HALF, Q_X2 = 5, 7
Q_LAYER2 = 4
S_Z3, S_Z3_STEP, S_H1_EARLY, S_H1, S_H2, S_Y = 15, 5, 23, 26, 30, 34
QUAD_J = [list(range(36, 39))] + [list(range(4 * q, 4 * q + 4)) for q in range(9)]
SLOTS = TILES * QUADS
RING = 4
GJ = F + 1
C1 = TOP1 // 128
C2 = TOP2 // 128
W1_PARTS = 3
TILES_BLOCK = MACROS * TILES

CHAIN_TILE = 20
A_TILE = 5
SUM_TILE = 4


def need(engine, sem, value):
    if isinstance(value, int) and value <= 0:
        return
    engine.wait_ge(sem, value)


def build(nc, table, ids, base_d, eye_d, w0_d, w1_d, w2_d, b1_d, cols_d, wt1_d, wt2_d, ctx_d, out):
    with ExitStack() as ctx:
        def sb(name, shape, dt=FP32):
            return ctx.enter_context(nc.sbuf_tensor(name, shape, dt))

        def bank(name):
            return ctx.enter_context(nc.psum_tensor(name, [128, 512], FP32))

        def sem(name):
            return ctx.enter_context(nc.semaphore(name))

        row_of = sb("row_of", [ROWS, MACROS * BLOCKS * GATHERS], INT32)
        base = sb("base", [ROWS, MACROS * BLOCKS * GATHERS], INT32)
        idx_all = sb("idx_all", [ROWS, MACROS * BLOCKS * GATHERS], INT32)
        idx = sb("idx", [ROWS, GATHERS], INT32)
        emb = sb("emb", [ROWS, 2, GATHERS * D])
        xx = sb("xx", [XX_ROWS, 2, COLS])
        eye = sb("eye", [2 * F, 2 * F])
        w0h = sb("w0h", [ROWS, GROUPS * H], FP32R)
        w0l = sb("w0l", [ROWS, GROUPS * H], FP32R)
        w1h = sb("w1h", [H, F * H], FP32R)
        w1l = sb("w1l", [H, F * H], FP32R)
        w2 = sb("w2", [H, F, H])
        g_all = sb("g_all", [H, GJ, BLOCK_B])
        w1_raw = g_all[:, 0:F, :].rearrange("k j h -> k (j h)")
        b1 = sb("b1", [128, H])
        cols = sb("cols", [128, C1 + 2 * C2 + 2])
        b2d = sb("b2d", [128, 1])
        wt1 = sb("wt1", [128, 3, TOP1])
        wt1c = sb("wt1c", [CTX, TOP1])
        wt2 = sb("wt2", [128, C1, TOP2])
        ctxt = sb("ctxt", [CTX, B])
        fac_a = sb("fac_a", [ROWS, 2, COLS])
        fac_b = sb("fac_b", [ROWS, GROUPS, COLS])
        w0_parts = fac_b[:].rearrange("p k c -> p (k c)")[:, 0:3 * GROUPS * H].rearrange("p (a h) -> p a h", a=3)
        w0 = w0_parts[:, 2]
        z0 = sb("z0", [ROWS, Z_RING, COLS])
        z0h = sb("z0h", [ROWS, Z_RING, COLS], FP32R)
        z0l = sb("z0l", [ROWS, Z_RING, COLS], FP32R)
        x1f = sb("x1f", [H, COLS])
        x1h = sb("x1h", [H, 2, COLS], FP32R)
        x1l = sb("x1l", [H, 2, COLS], FP32R)
        x0t = sb("x0t", [128, 2, TILES, GJ])
        bd = sb("bd", [128, 2, TILES, TILE_B, GJ])
        start = sb("start", [128, 2, 3, H])
        prod = sb("prod", [128, 2, 4, 4 * H])
        prod_sum = sb("prod_sum", [128, 2, 4 * H])
        chain = sb("chain", [128, 2, 4, H])
        total = sb("total", [128, 2, 4 * H])
        half = sb("half", [128, 2 * H])
        x2t = sb("x2t", [128, 2, H])
        z1 = sb("z1", [H, B])
        z2 = sb("z2", [H, BLOCK_B])
        z3 = sb("z3", [H, BLOCK_B])
        h1 = sb("h1", [128, C1, BLOCK_B])
        h2 = sb("h2", [128, C2, BLOCK_B])
        y = sb("y", [1, B])
        bt1 = [cols[:, c:c + 1] for c in range(C1)]
        bt2 = [cols[:, C1 + c:C1 + c + 1] for c in range(C2)]
        wt3 = [cols[:, C1 + C2 + c:C1 + C2 + c + 1] for c in range(C2)]
        b0 = cols[:, C1 + 2 * C2:C1 + 2 * C2 + 1]
        b2 = cols[:, C1 + 2 * C2 + 1:C1 + 2 * C2 + 2]

        p_u = [bank(f"p_u{i}") for i in range(RING)]
        p_x1 = bank("p_x1")
        p_g = bank("p_g")
        p_z = bank("p_z")
        p_h1 = bank("p_h1")

        idx_in = sem("idx_in")
        eye_in = sem("eye_in")
        w0_in = sem("w0_in")
        w1_in = [sem(f"w1_in{i}") for i in range(W1_PARTS)]
        w2_in = sem("w2_in")
        b1_in = sem("b1_in")
        cols_in = sem("cols_in")
        tower_in = sem("tower_in")
        idx_made = sem("idx_made")
        idx_copied = sem("idx_copied")
        gathered = [sem("gathered0"), sem("gathered1")]
        ones_set = sem("ones_set")
        w0_summed = sem("w0_summed")
        w0h_made = sem("w0h_made")
        w0l_made = sem("w0l_made")
        w1h_made = sem("w1h_made")
        w1l_made = sem("w1l_made")
        b2d_made = sem("b2d_made")
        x0_in = sem("x0_in")
        xx_in = sem("xx_in")
        xt_full = sem("xt_full")
        x0t_made = sem("x0t_made")
        a_in = [sem("a_in0"), sem("a_in1")]
        b_in = [sem(f"b_in{k}") for k in range(GROUPS)]
        z0_made = sem("z0_made")
        z0h_made = sem("z0h_made")
        z0l_made = sem("z0l_made")
        l0_added = sem("l0_added")
        x1f_made = sem("x1f_made")
        x1h_made = sem("x1h_made")
        x1l_made = sem("x1l_made")
        z1_made = sem("z1_made")
        bd_cleared = sem("bd_cleared")
        bd_in = [sem("bd_in0"), sem("bd_in1")]
        u_full = sem("u_full")
        a_scaled = sem("a_scaled")
        chained = sem("chained")
        summed = sem("summed")
        halved = sem("halved")
        x2_made = sem("x2_made")
        g_full = sem("g_full")
        g_kept = sem("g_kept")
        z3_full = sem("z3_full")
        z3_made = sem("z3_made")
        h1_full = sem("h1_full")
        h1_made = sem("h1_made")
        h2_full = sem("h2_full")
        h2_made = sem("h2_made")
        y_full = sem("y_full")
        y_made = sem("y_made")
        stored = sem("stored")

        block = ctx.enter_context(nc.Block())

        def over_blocks(engine, body):
            body(0, False, True)
            with engine.Fori(1, BLOCKS - 1) as n:
                body(n, True, True)
            body(BLOCKS - 1, True, False)

        @block.sync
        def _(sp):
            def spread(M, pair, par, first=False):
                sp.wait_ge(gathered[par], 16 * GATHERS * (pair + 1))
                at = 0
                for c in range(STACK):
                    sp.dma_start(xx[0:F, par, at:at + STAGE_COLS[c]],
                                 emb[c * F:(c + 1) * F, par, 0:STAGE_COLS[c]]).then_inc(x0_in, 16)
                    at += STAGE_COLS[c]
                sp.wait_ge(x0_in, 16 * STACK * (M + 1))
                for row in range(F, XX_ROWS, F):
                    rows = min(F, XX_ROWS - row)
                    sp.dma_start(xx[row:row + rows, par, :], xx[0:rows, par, :]).then_inc(xx_in, 16)
                sp.wait_ge(xx_in, 16 * STACK * (M + 1))
                for i in range(STACK):
                    row = -GROUPS * i % F
                    sp.dma_start(fac_a[i * F:(i + 1) * F, par, :], xx[row:row + F, par, :]).then_inc(a_in[par], 16)
                if first:
                    sp.wait_ge(w0l_made, 1)
                for k in range(GROUPS):
                    need(sp, z0_made, GROUPS * (M - 1) + k + 1)
                    sp.dma_start(fac_b[0:GROUP_ROWS[k], k, :], xx[k:k + GROUP_ROWS[k], par, :]).then_inc(b_in[k], 16)

            def place_bd(par):
                for b in range(TILE_B):
                    sp.dma_start(bd[b * D:(b + 1) * D, par, :, b, :], x0t[b * D:(b + 1) * D, par, :, :]
                                 ).then_inc(bd_in[par], 16)

            def body(n, has_prev, has_next):
                for m in range(MACROS):
                    M = n * MACROS + m
                    if has_next or m < MACROS - 2:
                        spread(M + 2, n * (MACROS // 2) + m // 2 + 1, m % 2)
                    elif m < MACROS - 1:
                        sp.wait_ge(z0_made, GROUPS * (M + 2))
                    if has_next or m < MACROS - 1:
                        need(sp, g_full, TILES * M)
                        place_bd((m + 1) % 2)

            sp.dma_start(row_of[:], ids).then_inc(idx_in, 16)
            sp.dma_start(base[:], base_d).then_inc(idx_in, 16)
            sp.dma_start(eye[:], eye_d).then_inc(eye_in, 16)
            sp.dma_start(fac_b[:].rearrange("p k c -> p (k c)")[:, 0:2 * GROUPS * H], w0_d).then_inc(w0_in, 16)
            step = F * H // W1_PARTS
            for i in range(W1_PARTS):
                sp.dma_start(w1_raw[:, i * step:(i + 1) * step], w1_d[:, i * step:(i + 1) * step]).then_inc(w1_in[i], 16)
            sp.dma_start(cols[:], cols_d).then_inc(cols_in, 16)
            sp.dma_start(b1[:], b1_d).then_inc(b1_in, 16)
            spread(0, 0, 0, first=True)
            spread(1, 0, 1)
            sp.wait_ge(x0t_made, 1)
            sp.wait_ge(bd_cleared, 1)
            place_bd(0)
            sp.dma_start(w2[:].rearrange("k j h -> k (j h)"), w2_d).then_inc(w2_in, 16)
            sp.dma_start(wt1[:], wt1_d[0:3 * 128, :].rearrange("(c p) n -> p c n", p=128)).then_inc(tower_in, 16)
            sp.dma_start(wt1c[:], wt1_d[3 * 128:3 * 128 + CTX, :]).then_inc(tower_in, 16)
            sp.dma_start(wt2[:], wt2_d.rearrange("(c p) n -> p c n", p=128)).then_inc(tower_in, 16)
            sp.dma_start(ctxt[:], ctx_d).then_inc(tower_in, 16)
            over_blocks(sp, body)
            sp.wait_ge(y_made, BLOCKS)
            sp.dma_start(out.rearrange("b a -> a b"), y[:]).then_inc(stored, 16)
            sp.wait_ge(stored, 16)

        @block.gpsimd
        def _(pool):
            def gather(par, g, index):
                rows = GATHER_ROWS[g]
                nc.gpsimd.indirect_dma_start(
                    out=emb[0:rows, par, g * D:(g + 1) * D], out_offset=None, in_=table,
                    in_offset=bass.IndirectOffsetOnAxis(ap=index[0:rows, g:g + 1], axis=0)).then_inc(gathered[par], 16)

            def body(n, has_prev, has_next):
                for tt in range(TILES_BLOCK):
                    T = n * TILES_BLOCK + tt
                    p, m, t = tt % 2, tt // TILES, tt % TILES
                    pool.wait_ge(a_scaled, A_TILE * T + 3)
                    need(pool, summed, SUM_TILE * (T - 1))
                    nc.gpsimd.tensor_tensor(out=prod_sum[:, p, :], in0=prod[:, p, 0, :], in1=prod[:, p, 1, :],
                                            op=ALU.add).then_inc(summed, 1)
                    for i in (2, 3):
                        pool.wait_ge(a_scaled, A_TILE * T + 2 + i)
                        pool.wait_ge(summed, SUM_TILE * T + i - 1)
                        nc.gpsimd.tensor_tensor(out=prod_sum[:, p, :], in0=prod_sum[:, p, :], in1=prod[:, p, i, :],
                                                op=ALU.add).then_inc(summed, 1)
                    pool.wait_ge(summed, SUM_TILE * T + 3)
                    pool.wait_ge(chained, CHAIN_TILE * (T + 1))
                    need(pool, halved, T - 1)
                    gathers = G_BATCH[t] if has_next or m < MACROS - G_AHEAD[t] else ()
                    if 0 in gathers:
                        M = n * MACROS + m + G_AHEAD[t]
                        pool.wait_ge(idx_copied, M - 1)
                        pool.wait_ge(xx_in, 16 * STACK * (M - 1))
                    nc.gpsimd.tensor_tensor(out=total[:, p, :], in0=prod_sum[:, p, :],
                                            in1=chain[:, p].rearrange("p a h -> p (a h)"),
                                            op=ALU.add).then_inc(summed, 1)
                    for g in gathers:
                        gather((m + G_AHEAD[t]) % 2, g, idx)

            pool.wait_ge(idx_made, 1)
            for M in (0, 1):
                for g in range(GATHERS):
                    gather(M, g, idx_all[:, GATHERS * M:GATHERS * (M + 1)])
            pool.wait_ge(xx_in, 16 * STACK)
            pool.wait_ge(idx_copied, 1)
            for t in (2, 3):
                for g in G_BATCH[t]:
                    gather(0, g, idx)
            over_blocks(pool, body)

        @block.scalar
        def _(act):
            def evac_x0t(M, pair, par):
                act.wait_ge(xt_full, M + 1)
                need(act, chained, CHAIN_TILE * TILES * (M - 1))
                need(act, a_scaled, A_TILE * TILES * (M - 1))
                need(act, bd_in[par], 16 * TILE_B * pair)
                nc.scalar.activation(x0t[:, par, :, 0:F],
                                     p_x1[:, 0:TILES * 2 * F].rearrange("p (t j) -> p t j", j=2 * F)[:, :, 0:F],
                                     ACT.Copy).then_inc(x0t_made, 1)

            def z0_high(M, k):
                rows = GROUP_ROWS[k]
                act.wait_ge(z0_made, GROUPS * M + k + 1)
                need(act, l0_added, GROUPS * M + max(k - Z_RING + 1, 0))
                nc.scalar.activation(z0h[0:rows, k % Z_RING, :], z0[0:rows, k % Z_RING, :], ACT.Copy).then_inc(z0h_made, 1)

            def evac_x1(M):
                act.wait_ge(l0_added, GROUPS * (M + 1))
                need(act, z1_made, M)
                need(act, x1l_made, M)
                need(act, x1h_made, M)
                nc.scalar.activation(x1f[:], p_x1[:], ACT.Identity, bias=b0).then_inc(x1f_made, 1)

            def make_x1h(M, par):
                act.wait_ge(x1f_made, M + 1)
                need(act, u_full, SLOTS * (M - 1))
                nc.scalar.activation(x1h[:, par, :], x1f[:], ACT.Copy).then_inc(x1h_made, 1)

            def keep_g(T, tt):
                act.wait_ge(g_full, T + 1)
                nc.scalar.activation(g_all[:, :, TILE_B * tt:TILE_B * (tt + 1)],
                                     p_g[:, 0:TILE_B * GJ].rearrange("h (b j) -> h j b", j=GJ),
                                     ACT.Copy).then_inc(g_kept, 1)

            def scale_quad(T, tt, q):
                p, par, t = tt % 2, (tt // TILES) % 2, tt % TILES
                act.wait_ge(u_full, QUADS * T + q + 1)
                if q == 0:
                    need(act, chained, CHAIN_TILE * (T - 2) + 4)
                    dst = start[:, p].rearrange("p a h -> p (a h)")
                else:
                    need(act, summed, SUM_TILE * (T - 2) + 3)
                    dst = prod[:, p, q // 2 - 1, :]
                u = p_u[(QUADS * tt + q) % RING]
                for i, j in enumerate(QUAD_J[q]):
                    last = nc.scalar.activation(dst[:, i * H:(i + 1) * H], u[:, i * H:(i + 1) * H], ACT.Copy,
                                                scale=x0t[:, par, t, j:j + 1])
                last.then_inc(a_scaled, 1)

            def tower_z(n):
                act.wait_ge(g_kept, TILES_BLOCK * (n + 1))
                nc.scalar.activation(z2[:], g_all[:, F, :], ACT.Copy).then_inc(z3_made, 1)
                act.wait_ge(z3_full, n + 1)
                nc.scalar.activation(z3[:], p_z[:, 0:BLOCK_B], ACT.Identity, bias=b2d[:]).then_inc(z3_made, 1)

            def tower_h1(n):
                act.wait_ge(h1_full, n + 1)
                for c in range(C1):
                    nc.scalar.activation(h1[:, c, :], p_h1[:, c * BLOCK_B:(c + 1) * BLOCK_B], ACT.Relu,
                                         bias=bt1[c]).then_inc(h1_made, 1)

            def tower_h2(n):
                act.wait_ge(h2_full, n + 1)
                for c in range(C2):
                    nc.scalar.activation(h2[:, c, :], p_z[:, c * BLOCK_B:(c + 1) * BLOCK_B], ACT.Relu,
                                         bias=bt2[c]).then_inc(h2_made, 1)

            def tower_y(n):
                act.wait_ge(y_full, n + 1)
                nc.scalar.activation(y[0:1, bass.ds(BLOCK_B * n, BLOCK_B)], p_z[0:1, 0:BLOCK_B],
                                     ACT.Copy).then_inc(y_made, 1)

            def body(n, has_prev, has_next):
                for m in range(MACROS):
                    M = n * MACROS + m
                    prepares = has_next or m < MACROS - 1
                    act.wait_ge(x0t_made, M + 1)
                    for s in range(SLOTS):
                        tt = m * TILES + s // QUADS
                        q = s % QUADS
                        T = n * TILES_BLOCK + tt
                        if prepares and s == S_COLUMNS:
                            evac_x0t(M + 1, n * (MACROS // 2) + (m + 1) // 2, (m + 1) % 2)
                        if prepares and s in S_HIGH:
                            z0_high(M + 1, S_HIGH.index(s))
                        if prepares and s == S_ADD[-1]:
                            evac_x1(M + 1)
                            make_x1h(M + 1, (m + 1) % 2)
                        if q == Q_LAYER2 and (has_prev or tt > 1):
                            if tt == 2:
                                need(act, z3_made, 2 * n)
                            keep_g(T - 2, (tt - 2) % TILES_BLOCK)
                        if has_prev and m == 0:
                            if s == S_H1_EARLY:
                                tower_z(n - 1)
                            if s == S_H1:
                                tower_h1(n - 1)
                            if s == S_H2:
                                tower_h2(n - 1)
                            if s == S_Y:
                                tower_y(n - 1)
                        if q % 2 == 0:
                            scale_quad(T, tt, q)

            act.wait_ge(w0_summed, 1)
            nc.scalar.activation(w0h[:], w0, ACT.Copy).then_inc(w0h_made, 1)
            step = F * H // W1_PARTS
            for i in range(W1_PARTS):
                act.wait_ge(w1_in[i], 16)
                nc.scalar.activation(w1h[:, i * step:(i + 1) * step], w1_raw[:, i * step:(i + 1) * step],
                                     ACT.Copy).then_inc(w1h_made, 1)
            act.wait_ge(cols_in, 16)
            nc.scalar.mul(b2d[:], b2, float(D)).then_inc(b2d_made, 1)
            act.wait_ge(b2d_made, 1)
            act.wait_ge(ones_set, 1)
            evac_x0t(0, 0, 0)
            for k in range(GROUPS):
                z0_high(0, k)
            evac_x1(0)
            make_x1h(0, 0)
            act.wait_ge(w1l_made, W1_PARTS)
            over_blocks(act, body)
            n = BLOCKS - 1
            for tt in (TILES_BLOCK - 2, TILES_BLOCK - 1):
                keep_g(TILES_BLOCK * n + tt, tt)
            tower_z(n)
            tower_h1(n)
            tower_h2(n)
            tower_y(n)

        @block.vector
        def _(dve):
            def copy_idx(M):
                nc.vector.tensor_copy(idx[:], idx_all[:, bass.ds(GATHERS * M, GATHERS)]).then_inc(idx_copied, 1)

            def product(M, pair, par, k):
                rows = GROUP_ROWS[k]
                dve.wait_ge(a_in[par], 16 * STACK * (pair + 1))
                dve.wait_ge(b_in[k], 16 * (M + 1))
                need(dve, z0l_made, GROUPS * M + max(k - Z_RING + 1, 0))
                nc.vector.tensor_tensor(out=z0[0:rows, k % Z_RING, :], in0=fac_b[0:rows, k, :], in1=fac_a[0:rows, par, :],
                                        op=ALU.mult).then_inc(z0_made, 1)

            def z0_low(M, k):
                rows = GROUP_ROWS[k]
                dve.wait_ge(z0h_made, GROUPS * M + k + 1)
                need(dve, l0_added, GROUPS * M + max(k - Z_RING + 1, 0))
                nc.vector.tensor_tensor(out=z0l[0:rows, k % Z_RING, :], in0=z0[0:rows, k % Z_RING, :],
                                        in1=z0h[0:rows, k % Z_RING, :].bitcast(FP32),
                                        op=ALU.subtract).then_inc(z0l_made, 1)

            def make_x1l(M, par):
                dve.wait_ge(x1h_made, M + 1)
                need(dve, u_full, SLOTS * (M - 1))
                nc.vector.tensor_tensor(out=x1l[:, par, :], in0=x1f[:], in1=x1h[:, par, :].bitcast(FP32),
                                        op=ALU.subtract).then_inc(x1l_made, 1)

            def sum_z1(M):
                dve.wait_ge(x1f_made, M + 1)
                nc.vector.tensor_reduce(out=z1[:, bass.ds(M * MACRO_B, MACRO_B)],
                                        in_=x1f[:].rearrange("h (b d) -> h b d", d=D),
                                        op=ALU.add, axis=AX.X).then_inc(z1_made, 1)

            def chain_quad(T, tt, q):
                p, par, t = tt % 2, (tt // TILES) % 2, tt % TILES
                k = q // 2
                dve.wait_ge(u_full, QUADS * T + q + 1)
                if k == 0:
                    dve.wait_ge(a_scaled, A_TILE * T + 1)
                    need(dve, summed, SUM_TILE * (T - 1))
                u = p_u[(QUADS * tt + q) % RING]
                for i, j in enumerate(QUAD_J[q]):
                    if k == 0:
                        add = b1[:] if i == 0 else start[:, p, i - 1, :]
                    else:
                        add = chain[:, p, i, :]
                        dve.wait_ge(chained, CHAIN_TILE * T + 4 * (k - 1) + i + 1)
                    nc.vector.scalar_tensor_tensor(
                        out=chain[:, p, i, :], in0=u[:, i * H:(i + 1) * H], scalar=x0t[:, par, t, j:j + 1],
                        in1=add, op0=ALU.mult, op1=ALU.add).then_inc(chained, 1)

            def fold_half(T, p):
                dve.wait_ge(summed, SUM_TILE * (T + 1))
                need(dve, x2_made, T)
                nc.vector.tensor_tensor(out=half[:], in0=total[:, p, 0:2 * H], in1=total[:, p, 2 * H:4 * H],
                                        op=ALU.add).then_inc(halved, 1)

            def fold_x2(T, p):
                dve.wait_ge(halved, T + 1)
                need(dve, g_full, T - 1)
                nc.vector.tensor_tensor(out=x2t[:, p, :], in0=half[:, 0:H], in1=half[:, H:2 * H],
                                        op=ALU.add).then_inc(x2_made, 1)

            def body(n, has_prev, has_next):
                for m in range(MACROS):
                    M = n * MACROS + m
                    prepares = has_next or m < MACROS - 1
                    dve.wait_ge(x0t_made, M + 1)
                    for s in range(SLOTS):
                        tt = m * TILES + s // QUADS
                        q = s % QUADS
                        T = n * TILES_BLOCK + tt
                        if q == Q_HALF and (has_prev or tt > 0):
                            fold_half(T - 1, (tt + 1) % 2)
                        if q == Q_X2 and (has_prev or tt > 0):
                            fold_x2(T - 1, (tt + 1) % 2)
                        if s == S_Z1:
                            sum_z1(M)
                        if s == S_INDEX and (has_next or m < MACROS - 3):
                            dve.wait_ge(gathered[m % 2], 16 * GATHERS * (n * (MACROS // 2) + m // 2 + 2))
                            copy_idx(M + 3)
                        for k in range(GROUPS):
                            if prepares and s == S_PAIR[k]:
                                product(M + 1, n * (MACROS // 2) + (m + 1) // 2, (m + 1) % 2, k)
                            if prepares and s == S_LOW[k]:
                                z0_low(M + 1, k)
                        if prepares and s == S_ADD[-1] + 1:
                            make_x1l(M + 1, (m + 1) % 2)
                        if q % 2 == 1:
                            chain_quad(T, tt, q)

            dve.wait_ge(idx_in, 32)
            nc.vector.tensor_tensor(out=idx_all[:], in0=row_of[:], in1=base[:], op=ALU.add).then_inc(idx_made, 1)
            nc.vector.memset(bd[:], 0.0).then_inc(bd_cleared, 1)
            nc.vector.memset(x0t[:], 1.0).then_inc(ones_set, 1)
            dve.wait_ge(w0_in, 16)
            nc.vector.tensor_tensor(out=w0, in0=w0_parts[:, 0], in1=w0_parts[:, 1], op=ALU.add).then_inc(w0_summed, 1)
            dve.wait_ge(w0h_made, 1)
            nc.vector.tensor_tensor(out=w0l[:], in0=w0, in1=w0h[:].bitcast(FP32),
                                    op=ALU.subtract).then_inc(w0l_made, 1)
            step = F * H // W1_PARTS
            for i in range(W1_PARTS):
                dve.wait_ge(w1h_made, i + 1)
                nc.vector.tensor_tensor(out=w1l[:, i * step:(i + 1) * step], in0=w1_raw[:, i * step:(i + 1) * step],
                                        in1=w1h[:, i * step:(i + 1) * step].bitcast(FP32),
                                        op=ALU.subtract).then_inc(w1l_made, 1)
            dve.wait_ge(b1_in, 16)
            dve.wait_ge(idx_made, 1)
            copy_idx(2)
            for k in range(GROUPS):
                product(0, 0, 0, k)
                if k:
                    z0_low(0, k - 1)
            z0_low(0, GROUPS - 1)
            make_x1l(0, 0)
            over_blocks(dve, body)
            T = TILES_BLOCK * BLOCKS - 1
            fold_half(T, T % 2)
            fold_x2(T, T % 2)

        @block.tensor
        def _(pe):
            def columns_on_partitions(M, par):
                pe.wait_ge(xx_in, 16 * STACK * (M + 1))
                need(pe, x1f_made, M)
                for t in range(TILES):
                    last = nc.tensor.transpose(p_x1[:, t * 2 * F:(t + 1) * 2 * F],
                                               xx[0:2 * F, par, t * 128:(t + 1) * 128], eye[:])
                last.then_inc(xt_full, 1)

            def add_group(M, k):
                rows = GROUP_ROWS[k]
                if k == 0:
                    pe.wait_ge(x0t_made, M + 1)
                wh, wl = w0h[0:rows, k * H:(k + 1) * H], w0l[0:rows, k * H:(k + 1) * H]
                zh, zl = z0h[0:rows, k % Z_RING, :], z0l[0:rows, k % Z_RING, :]
                pe.wait_ge(z0h_made, GROUPS * M + k + 1)
                nc.tensor.matmul(p_x1[:], wh, zh, start=(k == 0), stop=False)
                nc.tensor.matmul(p_x1[:], wl, zh, start=False, stop=False)
                pe.wait_ge(z0l_made, GROUPS * M + k + 1)
                nc.tensor.matmul(p_x1[:], wh, zl, start=False, stop=(k == GROUPS - 1)).then_inc(l0_added, 1)

            def quad(T, tt, q):
                par, t = (tt // TILES) % 2, tt % TILES
                if q % 2 == 0:
                    need(pe, a_scaled, A_TILE * T + q // 2 - 1)
                else:
                    need(pe, chained, CHAIN_TILE * T + 4 * (q // 2 - 1))
                js = QUAD_J[q]
                u = p_u[(QUADS * tt + q) % RING][:, 0:len(js) * H]
                xh = x1h[:, par, t * 128:(t + 1) * 128]
                xl = x1l[:, par, t * 128:(t + 1) * 128]
                wh = w1h[:, js[0] * H:(js[-1] + 1) * H]
                wl = w1l[:, js[0] * H:(js[-1] + 1) * H]
                nc.tensor.matmul(u, xh, wh, start=True, stop=False)
                nc.tensor.matmul(u, xh, wl, start=False, stop=False)
                nc.tensor.matmul(u, xl, wh, start=False, stop=True).then_inc(u_full, 1)

            def layer2(T, tt, pair, par):
                t, p = tt % TILES, tt % 2
                pe.wait_ge(x2_made, T + 1)
                pe.wait_ge(bd_in[par], 16 * TILE_B * (pair + 1))
                need(pe, g_kept, T)
                nc.tensor.matmul(p_g[:, 0:TILE_B * GJ], x2t[:, p, :], bd[:, par, t].rearrange("p b j -> p (b j)"),
                                 start=True, stop=True).then_inc(g_full, 1)

            def tower_z3(n, j0, j1):
                if j0 == 0:
                    pe.wait_ge(g_kept, TILES_BLOCK * (n + 1))
                    pe.wait_ge(w2_in, 16)
                for j in range(j0, j1):
                    last = nc.tensor.matmul(p_z[:, 0:BLOCK_B], w2[:, j, :], g_all[:, j, :],
                                            start=(j == 0), stop=(j == F - 1))
                if j1 == F:
                    last.then_inc(z3_full, 1)

            def tower_1_early(n):
                pe.wait_ge(tower_in, 64)
                pe.wait_ge(z1_made, MACROS * (n + 1))
                for c in range(C1):
                    o, h = p_h1[:, c * BLOCK_B:(c + 1) * BLOCK_B], slice(c * 128, (c + 1) * 128)
                    nc.tensor.matmul(o, wt1[:, 0, h], z1[:, bass.ds(BLOCK_B * n, BLOCK_B)], start=(c == 0), stop=False)
                    nc.tensor.matmul(o, wt1c[:, h], ctxt[:, bass.ds(BLOCK_B * n, BLOCK_B)], start=False, stop=False)

            def tower_1_late(n):
                pe.wait_ge(z3_made, 2 * (n + 1))
                for c in range(C1):
                    o, h = p_h1[:, c * BLOCK_B:(c + 1) * BLOCK_B], slice(c * 128, (c + 1) * 128)
                    nc.tensor.matmul(o, wt1[:, 1, h], z2[:], start=False, stop=False)
                    last = nc.tensor.matmul(o, wt1[:, 2, h], z3[:], start=False, stop=(c == C1 - 1))
                last.then_inc(h1_full, 1)

            def tower_2(n):
                for i in range(C1):
                    pe.wait_ge(h1_made, C1 * n + i + 1)
                    for c in range(C2):
                        last = nc.tensor.matmul(p_z[:, c * BLOCK_B:(c + 1) * BLOCK_B], wt2[:, i, c * 128:(c + 1) * 128],
                                                h1[:, i, :], start=(i == 0 and c == 0),
                                                stop=(i == C1 - 1 and c == C2 - 1))
                last.then_inc(h2_full, 1)

            def tower_3(n):
                pe.wait_ge(h2_made, C2 * (n + 1))
                for i in range(C2):
                    last = nc.tensor.matmul(p_z[0:1, 0:BLOCK_B], wt3[i], h2[:, i, :], start=(i == 0), stop=(i == C2 - 1))
                last.then_inc(y_full, 1)

            def prepare(M, par, s):
                if s == S_COLUMNS:
                    columns_on_partitions(M, par)
                for k in range(GROUPS):
                    if s == S_ADD[k]:
                        add_group(M, k)

            def body(n, has_prev, has_next):
                for m in range(MACROS):
                    M = n * MACROS + m
                    pe.wait_ge(x1h_made, M + 1)
                    pe.wait_ge(x1l_made, M + 1)
                    for s in range(SLOTS):
                        tt = m * TILES + s // QUADS
                        q = s % QUADS
                        T = n * TILES_BLOCK + tt
                        if has_next or m < MACROS - 1:
                            prepare(M + 1, (m + 1) % 2, s)
                        if q == Q_LAYER2 and (has_prev or tt > 1):
                            mm = (tt - 2) // TILES
                            layer2(T - 2, (tt - 2) % TILES_BLOCK, n * (MACROS // 2) + mm // 2, mm % 2)
                        if has_prev and m == 0:
                            if S_Z3 <= s < S_H1_EARLY:
                                tower_z3(n - 1, S_Z3_STEP * (s - S_Z3), min(F, S_Z3_STEP * (s - S_Z3 + 1)))
                            if s == S_H1_EARLY:
                                tower_1_early(n - 1)
                            if s == S_H1:
                                tower_1_late(n - 1)
                            if s == S_H2:
                                tower_2(n - 1)
                            if s == S_Y:
                                tower_3(n - 1)
                        quad(T, tt, q)

            pe.wait_ge(eye_in, 16)
            pe.wait_ge(w0l_made, 1)
            columns_on_partitions(0, 0)
            for k in range(GROUPS):
                add_group(0, k)
            pe.wait_ge(w1l_made, W1_PARTS)
            over_blocks(pe, body)
            n = BLOCKS - 1
            T = TILES_BLOCK * BLOCKS - 1
            pair = MACROS * BLOCKS // 2 - 1
            layer2(T - 1, TILES_BLOCK - 2, pair, 1)
            tower_1_early(n)
            layer2(T, TILES_BLOCK - 1, pair, 1)
            tower_z3(n, 0, F)
            tower_1_late(n)
            tower_2(n)
            tower_3(n)


def kernel(**inputs):
    import numpy as np
    import concourse.bacc as bacc
    from concourse.bass_utils import run_bass_kernel_spmd

    x = {k: np.asarray(v) for k, v in inputs.items()}
    f32 = np.float32
    w0 = x["L0_rec_W0"].reshape(H, F, F)
    w0ab = np.zeros((STACK, F, 2, GROUPS, H), f32)
    for k in range(GROUPS):
        for i in range(STACK):
            a, b = (np.arange(F) - GROUPS * i) % F, (np.arange(F) + k) % F
            if SHIFT[k][i] < SHIFTS:
                w0ab[i, :, 0, k] = w0[:, a, b].T
            if 0 < SHIFT[k][i] < SHIFTS:
                w0ab[i, :, 1, k] = w0[:, b, a].T
    w0ab = w0ab.reshape(ROWS, 2 * GROUPS * H)
    w_j = {n: x[f"L0_rec_W{n}"].reshape(H, F, H).transpose(2, 1, 0).reshape(H, F * H) for n in (1, 2)}
    cols = np.concatenate([x["b_top1"].reshape(C1, 128).T, x["b_top2"].reshape(C2, 128).T,
                           x["W_top3"].reshape(C2, 128).T, x["L0_rec_b0"][:, None], x["L0_rec_b2"][:, None]], axis=1)
    sizes = [x[f"tbl_{f}"].shape[0] for f in range(F)]
    samples = np.pad(x["ids"].reshape(-1, MACRO_B, F), ((0, 0), (0, STACK * GATHERS - MACRO_B), (0, 0)))
    ids = samples.reshape(-1, STACK, GATHERS, F).transpose(1, 3, 0, 2).reshape(ROWS, -1)
    first_row = np.concatenate([[0], np.cumsum(sizes)[:-1]]).astype(np.int32)
    base = np.broadcast_to(np.tile(first_row, STACK)[:, None], ids.shape)
    arrays = {
        "table": np.concatenate([x[f"tbl_{f}"] for f in range(F)]),
        "ids": ids, "base": base,
        "eye": np.eye(2 * F, dtype=f32),
        "w0ab": w0ab, "w1": w_j[1], "w2": w_j[2],
        "b1": np.broadcast_to(x["L0_rec_b1"], (128, H)),
        "cols": cols, "wt1": x["W_top1"], "wt2": x["W_top2"], "ctx": x["dense_ctx"].T,
    }
    arrays = {k + "_in": np.ascontiguousarray(v) for k, v in arrays.items()}
    nc = bacc.Bacc("TRN2", target_bir_lowering=False, num_devices=1)

    def declare(name, a):
        return nc.dram_tensor(name, a.shape, mybir.dt.from_np(a.dtype), kind="ExternalInput").ap()

    args = [declare(name, a) for name, a in arrays.items()]
    out = nc.dram_tensor("out", (B, 1), FP32, kind="ExternalOutput").ap()
    build(nc, *args, out)
    result = run_bass_kernel_spmd(nc, [arrays], core_ids=[0])
    return result.results[0]["out"]
```
